# Optimizing a Trainium2 kernel written in Bass

```python
import numpy as np
import jax
import jax.numpy as jnp

def _softmax(x, axis=-1):
    return jax.nn.softmax(x, axis=axis)

def _gelu(x):
    return jax.nn.gelu(x, approximate=True)

def _silu(x):
    return jax.nn.silu(x)

def _sigmoid(x):
    return jax.nn.sigmoid(x)

def _layernorm(x, axis=-1, eps=1e-05):
    m = jnp.mean(x, axis=axis, keepdims=True)
    v = jnp.var(x, axis=axis, keepdims=True)
    return (x - m) / jnp.sqrt(v + eps)

def _scatter_add(tgt, idx, src, axis=0):
    return tgt.at[idx].add(src)

def _segment_sum(src, seg, n):
    return jax.ops.segment_sum(src, seg, n)
kernel_name = 'mk_gnn_preln_d2_gnn_r64_c9d58c'

def setup_inputs(seed: int=0):
    np.random.seed(seed)
    _w = jnp.asarray

    def _rec_inputs():
        import jax
        import jax.numpy as jnp
        _gk = jax.random.key(seed)
        x = -0.0001006 + 1 * jax.random.normal(jax.random.fold_in(_gk, 1), (100000, 96), jnp.float32)
        src = jax.random.randint(jax.random.fold_in(_gk, 2), (25000,), 0, 100000, jnp.int32)
        dst = jax.random.randint(jax.random.fold_in(_gk, 3), (25000,), 0, 100000, jnp.int32)
        _o = jnp.argsort(dst, stable=True)
        src = src[_o]
        dst = dst[_o]
        edge_attr_64 = 0.000189758 + 1.00013 * jax.random.normal(jax.random.fold_in(_gk, 11), (25000, 64), jnp.float32)
        return (x, src, dst, edge_attr_64)
    x, src, dst, edge_attr_64 = _rec_inputs()

    def _L0_gnn_setup():
        import jax, jax.numpy as jnp
        import numpy as np
        N_NODES = 50000
        N_EDGES = 12500
        D = 96
        LN_EPS = 1e-05

        def _layer(h, src, dst, norm, n_nodes, W, b, g, be):
            h = h @ W
            msg = h[src] * norm[:, None]
            h = jax.ops.segment_sum(msg, dst, num_segments=n_nodes) + b
            h = jnp.tanh(h)
            mu = jnp.mean(h, axis=-1, keepdims=True)
            var = jnp.mean(jnp.square(h - mu), axis=-1, keepdims=True)
            h = (h - mu) * jax.lax.rsqrt(var + LN_EPS)
            return h * g + be
        key = jax.random.key(seed)
        ks = jax.random.split(key, 4)
        x = jax.random.normal(ks[0], (N_NODES, D), dtype=jnp.float32)
        edge_index = jax.random.randint(ks[1], (2, N_EDGES), 0, N_NODES, dtype=jnp.int64)
        scale = 1.0 / np.sqrt(D)
        W0 = jax.random.normal(ks[2], (D, D), dtype=jnp.float32) * scale
        W1 = jax.random.normal(ks[3], (D, D), dtype=jnp.float32) * scale
        b0 = jnp.zeros((D,), jnp.float32)
        b1 = jnp.zeros((D,), jnp.float32)
        g0 = jnp.ones((D,), jnp.float32)
        g1 = jnp.ones((D,), jnp.float32)
        be0 = jnp.zeros((D,), jnp.float32)
        be1 = jnp.zeros((D,), jnp.float32)
        return {'x': x, 'edge_index': edge_index, 'W0': W0, 'b0': b0, 'g0': g0, 'be0': be0, 'W1': W1, 'b1': b1, 'g1': g1, 'be1': be1}
    _L0_gnn_all = _L0_gnn_setup()
    _L0_gnn_in = {k: v for k, v in _L0_gnn_all.items() if k in ('W0', 'b0', 'g0', 'be0', 'W1', 'b1', 'g1', 'be1')}
    del _L0_gnn_all

    def _L1_gnn_setup():
        import jax, jax.numpy as jnp
        import numpy as np
        N, E = (50000, 12500)
        NODE_DIM, EDGE_DIM = (96, 64)
        IN_DIM = 2 * NODE_DIM + EDGE_DIM
        key = jax.random.key(seed)
        k = jax.random.split(key, 7)
        h = jax.random.normal(k[0], (N, NODE_DIM), dtype=jnp.float32)
        edge_index = jax.random.randint(k[1], (2, E), 0, N, dtype=jnp.int64)
        edge_attr = jax.random.normal(k[2], (E, EDGE_DIM), dtype=jnp.float32)
        s = 1.0 / np.sqrt(IN_DIM)
        W_e = jax.random.uniform(k[3], (IN_DIM, NODE_DIM), jnp.float32, -s, s)
        b_e = jax.random.uniform(k[4], (NODE_DIM,), jnp.float32, -s, s)
        W_n = jax.random.uniform(k[5], (IN_DIM, NODE_DIM), jnp.float32, -s, s)
        b_n = jax.random.uniform(k[6], (NODE_DIM,), jnp.float32, -s, s)
        return {'h': h, 'edge_index': edge_index, 'edge_attr': edge_attr, 'W_e': W_e, 'b_e': b_e, 'W_n': W_n, 'b_n': b_n}
    _L1_gnn_all = _L1_gnn_setup()
    _L1_gnn_in = {k: v for k, v in _L1_gnn_all.items() if k in ('W_e', 'b_e', 'W_n', 'b_n')}
    del _L1_gnn_all
    return {'x': x, 'src': src, 'dst': dst, 'edge_attr_64': edge_attr_64, 'L0_gnn_W0': _L0_gnn_in['W0'], 'L0_gnn_b0': _L0_gnn_in['b0'], 'L0_gnn_g0': _L0_gnn_in['g0'], 'L0_gnn_be0': _L0_gnn_in['be0'], 'L0_gnn_W1': _L0_gnn_in['W1'], 'L0_gnn_b1': _L0_gnn_in['b1'], 'L0_gnn_g1': _L0_gnn_in['g1'], 'L0_gnn_be1': _L0_gnn_in['be1'], 'L1_gnn_W_e': _L1_gnn_in['W_e'], 'L1_gnn_b_e': _L1_gnn_in['b_e'], 'L1_gnn_W_n': _L1_gnn_in['W_n'], 'L1_gnn_b_n': _L1_gnn_in['b_n']}

def reference(x, src, dst, edge_attr_64, L0_gnn_W0, L0_gnn_b0, L0_gnn_g0, L0_gnn_be0, L0_gnn_W1, L0_gnn_b1, L0_gnn_g1, L0_gnn_be1, L1_gnn_W_e, L1_gnn_b_e, L1_gnn_W_n, L1_gnn_b_n):
    import jax
    import jax.numpy as jnp

    def _L0_gnn_ref(x, edge_index, W0, b0, g0, be0, W1, b1, g1, be1):
        import jax, jax.numpy as jnp
        import numpy as np
        N_NODES = 50000
        N_EDGES = 12500
        D = 96
        LN_EPS = 1e-05

        def _layer(h, src, dst, norm, n_nodes, W, b, g, be):
            h = h @ W
            msg = h[src] * norm[:, None]
            h = jax.ops.segment_sum(msg, dst, num_segments=n_nodes) + b
            h = jnp.tanh(h)
            mu = jnp.mean(h, axis=-1, keepdims=True)
            var = jnp.mean(jnp.square(h - mu), axis=-1, keepdims=True)
            h = (h - mu) * jax.lax.rsqrt(var + LN_EPS)
            return h * g + be
        n = x.shape[0]
        loops = jnp.arange(n, dtype=edge_index.dtype)
        src = jnp.concatenate([edge_index[0], loops])
        dst = jnp.concatenate([edge_index[1], loops])
        deg = jax.ops.segment_sum(jnp.ones(src.shape, x.dtype), dst, num_segments=n)
        dis = jax.lax.rsqrt(deg)
        norm = dis[src] * dis[dst]
        h = _layer(x, src, dst, norm, n, W0, b0, g0, be0)
        h = _layer(h, src, dst, norm, n, W1, b1, g1, be1)
        return h

    def _L1_gnn_ref(h, edge_index, edge_attr, W_e, b_e, W_n, b_n):
        import jax, jax.numpy as jnp
        import numpy as np
        N, E = (50000, 12500)
        NODE_DIM, EDGE_DIM = (96, 64)
        IN_DIM = 2 * NODE_DIM + EDGE_DIM
        src, dst = (edge_index[0], edge_index[1])
        concat = jnp.concatenate([h[src], h[dst], edge_attr], axis=-1)
        gates = jax.nn.sigmoid(concat @ W_e + b_e)
        messages = jax.nn.softplus(concat @ W_n + b_n)
        gated = gates * messages
        n = h.shape[0]
        h_new = jax.ops.segment_sum(gated, dst, num_segments=n)
        edge_count = jax.ops.segment_sum(jnp.ones((dst.shape[0],), h.dtype), dst, num_segments=n)
        edge_count = jnp.clip(edge_count, 1.0, None)[:, None]
        return h + h_new / edge_count
    edge_index = jnp.stack([src, dst])
    h = jnp.maximum(_layernorm(x, axis=-1), 0.0)
    x = x + _L0_gnn_ref(h, edge_index, L0_gnn_W0, L0_gnn_b0, L0_gnn_g0, L0_gnn_be0, L0_gnn_W1, L0_gnn_b1, L0_gnn_g1, L0_gnn_be1)
    h = jnp.maximum(_layernorm(x, axis=-1), 0.0)
    x = x + _L1_gnn_ref(h, edge_index, edge_attr_64, L1_gnn_W_e, L1_gnn_b_e, L1_gnn_W_n, L1_gnn_b_n)
    return x

_drawn_inputs = setup_inputs


def setup_inputs(seed=0):
    import zlib

    import numpy as np

    out = dict(_drawn_inputs(seed))
    spreads = {'L0_gnn_b0': (0.0, 0.1),
     'L0_gnn_g0': (1.0, 0.2),
     'L0_gnn_be0': (0.0, 0.1),
     'L0_gnn_b1': (0.0, 0.1),
     'L0_gnn_g1': (1.0, 0.2),
     'L0_gnn_be1': (0.0, 0.1)}
    factors = {'edge_attr_64': 2.895, 'L1_gnn_W_e': 3.101, 'L1_gnn_b_e': 49.338, 'L1_gnn_b_n': 22.065}
    for name, (base, spread) in spreads.items():
        noise = np.random.default_rng([zlib.crc32(name.encode()), seed]).standard_normal(out[name].shape)
        drawn = base * np.exp(spread * noise) if base else spread * noise
        out[name] = jnp.asarray(drawn.astype(out[name].dtype))
    for name, factor in factors.items():
        out[name] = (out[name] * factor).astype(out[name].dtype)
    return out
```

```python
from contextlib import ExitStack
from itertools import count

import numpy as np
import concourse.bass as bass
from concourse import mybir

F32 = mybir.dt.float32
I32 = mybir.dt.int32
ALU = mybir.AluOpType
ACT = mybir.ActivationFunctionType
AX = mybir.AxisListType

P = 128
N, D = 100000, 96
E, DE = 25000, 64
G = 4
R = 4
DA = D + 1
T = -(-E // P)
ES = P * T
FIX = ES
ROWS = ES + P
EU = T // G
NU = -(-N // (P * G))
FILL = 125
LAST = N - P * G
SKIP = 1 << 20
EPS = 1e-5

PUT, TAKE = 0, 52
S1 = 108
S2 = S1 + EU + 3
END = S2 + EU + 6
END3 = EU + 4
RANKED = 3 + P * (5 * (T // 7) + 2)
assert T % 7 == 0 and T % G == 0 and EU % R == 1 and not any(s % R for s in (PUT, TAKE, S1, S2))
SEGMENTS = [("steps", 0, 8), ("loop", 8, 48), ("steps", 48, 60), ("loop", 60, 100),
            ("steps", 100, S1 + 8), ("loop", S1 + 8, S1 + 48), ("steps", S1 + 48, S2 + 8),
            ("loop", S2 + 8, NU - 4), ("steps", NU - 4, END)]
SEGMENTS3 = [("steps", 0, 8), ("loop", 8, 44), ("steps", 44, END3)]


class At:

    def __init__(self, j, c, span=(0, 1)):
        self.j, self.c, self.span = j, c, span

    def __add__(self, k):
        return At(self.j, self.c + k, self.span)

    def __sub__(self, k):
        return self + -k

    @property
    def slot(self):
        return self.c % R

    def times(self, a, b=0):
        return a * self.c + b if self.j is None else self.j * (R * a) + (a * self.c + b)

    def laps(self, a, b=0):
        return a * (self.c // R) + b if self.j is None else self.j * a + (a * (self.c // R) + b)

    def within(self, n, first=0):
        lo, hi = (R * k + self.c for k in (self.span[0], self.span[1] - 1))
        yes = [first <= v < n for v in (lo, hi)]
        assert yes[0] == yes[1] and not (lo < first and hi >= n)
        return yes[0]

    @property
    def exists(self):
        return self.j is not None or self.c >= 0

    @property
    def number(self):
        return self.c if self.j is None else None


class Count:

    def __init__(self, sem, base=0):
        self.sem, self.base = sem, base

    def at(self, value):
        return value + self.base

    def upto(self, u, per=1):
        return u.times(per, per + self.base)

    def again(self, total):
        return Count(self.sem, self.base + total)


class Slots:

    def __init__(self, sems, base=(0,) * R):
        self.sems, self.base = sems, base

    def __getitem__(self, k):
        return self.sems[k]

    def upto(self, u, each=16, last=None):
        return u.laps(each, (each if last is None else last) + self.base[u.slot])

    def all(self, k, units, each=16):
        return each * len(range(k, units, R)) + self.base[k]

    def again(self, *uses):
        base = [b + sum(each * len([u for u in range(lo, hi) if u % R == k]) for lo, hi, each in uses)
                for k, b in enumerate(self.base)]
        return Slots(self.sems, base)


def run_steps(eng, step, segments=SEGMENTS):
    for kind, lo, hi in segments:
        if kind == "steps":
            for s in range(lo, hi):
                step(At(None, s))
        else:
            assert lo % R == 0 and hi % R == 0
            with eng.Fori(lo // R, hi // R) as j:
                for c in range(R):
                    step(At(j, c, (lo // R, hi // R)))


def build(nc, x, src, dst, edge_attr, W0, b0, g0, be0, W1, b1, g1, be1, W_e, b_e, W_n, b_n, out):
    with ExitStack() as ctx:
        def sb(name, shape, dt=F32):
            return ctx.enter_context(nc.sbuf_tensor(name, shape, dt))

        def sem(name):
            return Count(ctx.enter_context(nc.semaphore(name)))

        def ring_sems(name):
            return Slots([ctx.enter_context(nc.semaphore(f"{name}{k}")) for k in range(R)])

        def dram(name, shape, dt=F32):
            return nc.dram_tensor(name, shape, dt).ap()

        dst_sorted = dram("dst_sorted", [1, ES + 2], I32)
        src_sorted = dram("src_sorted", [1, ES], I32)
        attr_sorted = dram("attr_sorted", [ES, DE])
        attr_given = dram("attr_given", [ES, DE])
        node_tab = dram("node_tab", [N, 2])
        sum_tab = [dram(f"sum_tab{k}", [ES, D]) for k in range(3)]
        z_src = dram("z_src", [ES, D])
        h_src = dram("h_src", [ES, D])
        x_dst = dram("x_dst", [ROWS, D])
        z_dst = dram("z_dst", [ROWS, D])
        h_dst = dram("h_dst", [ROWS, D])
        o_dst = dram("o_dst", [ROWS, D])

        def edge_units(table, width=D):
            return table[0:ES].rearrange("(p t) d -> p (t d)", p=P)

        ident = sb("ident", [P, P])
        idle = sb("idle", [P, 2, 8, R])
        w0 = sb("w0", [DA, D])
        w1n = sb("w1n", [DA, D])
        w1z = sb("w1z", [DA, D])
        wa = sb("wa", [DA, 2 * D])
        wb = sb("wb", [D, 2 * D])
        wc = sb("wc", [DE, 2 * D])
        g0b, be0b, g1b, be1b = (sb(n, [P, D]) for n in ("g0b", "be0b", "g1b", "be1b"))
        g0c = sb("g0c", [D, 1])
        centre = sb("centre", [D, DA])
        pick = sb("pick", [D, DA])
        w1g = sb("w1g", [DA, D])
        mhalf = sb("mhalf", [P, 3 * G])
        zeros = sb("zeros", [P, 2 * D])
        pads = sb("pads", [1, 3, ES - E + 2], I32)
        fill = sb("fill", [P, N // FILL])

        di = sb("di", [P, 3, T], I32)
        si = sb("si", [P, T], I32)
        df = sb("df", [P, 3, T])
        same = sb("same", [P, T])
        rep = sb("rep", [P, T])
        in_first = sb("in_first", [P, T])
        in_last = sb("in_last", [P, T])
        col = sb("col", [P, T])
        base = sb("base", [P, T])
        tmpa = sb("tmpa", [P, T])
        iota_i = sb("iota_i", [P, T], I32)
        part_i = sb("part_i", [P, P], I32)
        part = sb("part", [P, P])
        cols = sb("cols", [P, 16])
        first_row = sb("first_row", [P, P])
        eq_ff = sb("eq_ff", [P, P])
        eq_lf = sb("eq_lf", [P, P])
        ends_cnt = sb("ends_cnt", [P, 2])
        idx = sb("idx", [P, T, 5], I32)
        idx_fix = sb("idx_fix", [P, 4], I32)
        pay = sb("pay", [P, T, 2])
        pay_fix = sb("pay_fix", [P, 2])
        seen = sb("seen", [P, T, 2])
        fac = sb("fac", [P, T, 5])
        fac_fix = sb("fac_fix", [P, 5])
        degs = sb("degs", [P, 2 * T + 1])
        dis = sb("dis", [P, 2 * T + 1])
        dis_t = sb("dis_t", [P, 2 * T + 1])

        falls = sb("falls", [1, 1], I32)
        rank_i = sb("rank_i", [P, 2, T], I32)

        def ring(name, width=D, slots=R, dt=F32, g=G):
            return sb(name, [P, slots, g, width], dt)

        class Chain:

            def __init__(self, name, sets):
                self.x = ring(name + "_x") if name != "e2" else edge.x
                self.u = ring(name + "_u", DA, 2)
                self.a1 = ring(name + "_a1", DA, 2) if name != "e2" else None
                self.a2 = ring(name + "_a2", D, 2)
                self.x1 = ring(name + "_x1") if name != "e2" else edge.x1
                self.h = ring(name + "_h", D, 4)
                self.o = ring(name + "_o") if name != "edge" else None
                self.bn = [sb(f"{name}_bn{k}", [P, sets, 6]) for k in "ab"]
                self.mean = [sb(f"{name}_mean{k}", [P, 2, sets]) for k in "ab"]
                self.var = [sb(f"{name}_var{k}", [P, 2, sets]) for k in "ab"]
                self.rstd = [sb(f"{name}_rstd{k}", [P, 2, sets]) for k in "ab"]
                self.tmp = sb(name + "_tmp", [P, 3, sets])
                self.nb = sb(name + "_nb", [P, 2, G])
                self.z = sb(name + "_z", [P, G, D])
                self.xb = sb(name + "_xb", [P, G, D])
                self.loaded = (ring_sems(name + "_loaded") if name != "e2"
                               else xd_stored.again((0, EU + 1, 16)))
                if name != "edge":
                    self.o_stored = ring_sems(name + "_o_stored")
                self.s_stats = sem(name + "_stats")
                self.s_var = [sem(name + "_var_a")]
                self.s_rstd = [sem(name + "_rstd_a")]
                self.s_u, self.s_x1, self.s_nb = (sem(f"{name}_{k}") for k in ("u", "x1", "nb"))
                self.s_h = sem(name + "_h") if name != "e2" else s_rowin.again(1)
                self.s_z = sem(name + "_z") if name != "e2" else s_cntin.again(1)
                self.s_tp1, self.s_ut1, self.s_q1 = (sem(f"{name}_{k}") for k in ("tp1", "ut1", "q1"))
                self.s_a2 = sem(name + "_a2")
                if name != "e2":
                    self.s_var.append(sem(name + "_var_b"))
                    self.s_rstd.append(sem(name + "_rstd_b"))
                    self.s_a1_std, self.s_a1 = sem(name + "_a1_std"), sem(name + "_a1")
                    self.s_tp2, self.s_ut2, self.s_q2 = (sem(f"{name}_{k}") for k in ("tp2", "ut2", "q2"))
                if name != "edge":
                    self.s_o = sem(name + "_o") if name != "e2" else s_w1in.again(1)

        node = Chain("node", 2 * G)
        edge = Chain("edge", 3 * G)
        s_w1in, s_rowin, s_cntin, s_const = (sem(n) for n in ("w1_in", "row_in", "cnt_in", "const"))
        xd_stored = ring_sems("xd_st")
        e2 = Chain("e2", 2 * G)

        xd = ring("xd")
        ud = sb("ud", [P, G, D])
        bd = ring("bd", DA, 2)
        ad = ring("ad", D, 2)
        msg = sb("msg", [P, G, D])
        sums = ring("sums")
        zs = ring("zs")
        zd = ring("zd")
        coef = sb("coef", [P, 2, 2, G])
        fct = sb("fct", [P, 2, G, 5])
        zt = sb("zt", [P, 2, G, D])
        ends = sb("ends", [P, 3, D])
        ixr = sb("ixr", [P, R, G, 5], I32)
        ixr3 = sb("ixr3", [P, R, G, 5], I32)
        payr = sb("payr", [P, R, G, 2])
        seenr = sb("seenr", [P, R, G, 2])
        zs2 = ring("zs2")
        zd2 = ring("zd2")
        sums2 = ring("sums2")
        fct2 = sb("fct2", [P, 2, G, 5])
        hs3 = ring("hs3", DA)
        at3 = edge.h[:, :, :, 0:DE]
        fct3 = sb("fct3", [P, 2, G, 5])
        hd3, o3, res3, sums3 = xd, zs, zd, sums
        eg3, ab3, ex3, ln3, gt3 = node.z, node.xb, edge.z, edge.xb, e2.z
        firsts, masked, masked2 = (msg[:, :, :].rearrange("p g d -> p (g d)")[:, k * P:(k + 1) * P]
                                   for k in range(3))
        own_t = [b[:, :, :, :].rearrange("p s g d -> p (s g d)")[:, 0:7 * T].rearrange(
            "p (k t) -> p k t", k=7) for b in (sums, sums2, zs)]
        others_f, others_no, own_no, rank_f = (
            zd[:, :, :, :].rearrange("p s g d -> p (s g d)")[:, k * T:(k + 1) * T] for k in range(4))
        others_i = iota_i[:, :]
        scan, scanb = (b[:, :, :, :].rearrange("p s g d -> p (s g d)")[:, 0:4 * T].rearrange(
            "p (k t) -> p k t", k=4) for b in (zs2, zd2))

        ut = sb("ut", [DA, 4, P * G])
        TPS = [ctx.enter_context(nc.psum_tensor(f"tp{k}", [P, P * G], F32)) for k in range(4)]
        QALL = ctx.enter_context(nc.psum_tensor("q", [P, 4 * 512], F32))
        QS = [QALL[:, 512 * k:512 * k + 512] for k in range(4)]

        def qv(k, g=None):
            v = QS[k][:, 0:G * D].rearrange("p (g d) -> p g d", g=G)
            return v if g is None else v[:, g, :]

        s_staged, s_w, s_wz, s_ident = (
            sem(n) for n in ("staged", "weights", "wz", "ident_ready"))
        s_prep = sem("prep")
        s_falls, s_falls_sum, s_order = sem("falls"), sem("falls_sum"), sem("order_known")
        s_others, s_others_used, s_rank = sem("others_in"), sem("others_used"), sem("rank")
        s_given, s_rows_in, s_resorted, s_reloaded = (
            sem(n) for n in ("attr_given", "attr_rows_in", "resorted", "reloaded"))
        s_sort_copied = sem("sort_copied")
        s_wmm, s_w1n = sem("wmm"), sem("w1n_ready")
        s_edges = sem("edges_loaded")
        s_row, s_cnt = sem("row_ready"), sem("cnt_ready")
        s_idx, s_tab0, s_fac = sem("idx_ready"), sem("tab_zeroed"), sem("fac_ready")
        s_copied, s_put, s_got = sem("ix_copied"), ring_sems("tab_put"), ring_sems("tab_got")
        s_putfix = sem("tab_put_fix")
        s_seen = sem("seen_ready")
        s_deg, s_dis = sem("deg_ready"), sem("dis_ready")
        s_zero = sem("zeroed")
        xd_loaded = ring_sems("xd_loaded")
        sum_stored, zs_stored, zd_stored, hs_stored = (
            ring_sems(n) for n in ("sum_st", "zs_st", "zd_st", "hs_st"))
        s_ix1, s_fct, s_msg, s_sum, s_ud, s_bd, s_ad, s_zs, s_zd, s_zt, s_ztd, s_udt, s_utd, s_qd = (
            sem(n) for n in ("ix1", "fct", "msg", "sum", "ud", "bd_ready", "ad_ready",
                             "zs_ready", "zd_ready", "zt", "ztd", "tpd", "utd", "qd"))
        s_ends, s_tot = sem("ends_in"), sem("tot")
        sum2_stored, hd_stored = ring_sems("sum2_st"), ring_sems("hd_st")
        s_ix2, s_fct2, s_msg2, s_sum2 = (c.again(1) for c in (s_wmm, s_row, s_cnt, s_w1n))
        zs2_laid = s_put.again((0, EU, 16 * G))
        zs2_loaded = zs_stored.again((0, EU, 16))
        zd2_loaded = zd_stored.again((0, EU + 1, 16))
        hs3_laid = zs2_laid.again((0, EU, 16 * G))
        hd3_got = s_got.again((0, EU, 16 * G))
        out_put = xd_loaded.again((0, EU, 16 * G), (EU, EU + 1, 16))
        hs3_loaded = hs_stored.again((0, EU, 16))
        rest3_loaded = hd_stored.again((0, EU + 1, 16))
        sum3_stored = sum_stored.again((0, EU, 16))
        s_ix3, s_ixput3 = s_ix1.again(EU), s_copied.again(3 * EU)
        s_tp3, s_ut3, s_q3 = (c.again(EU) for c in (edge.s_tp1, edge.s_ut1, edge.s_q1))
        s_exp3, s_abs3, s_ea3, s_ln3 = (c.again(EU) for c in (edge.s_a1, edge.s_ut2, edge.s_a2, edge.s_h))
        s_m3, s_rc3, s_gt3, s_e13 = (c.again(k) for c, k in (
            (s_msg, EU), (edge.s_u, EU), (edge.s_x1, EU), (s_ud, EU + 1)))
        s_sum3, s_fct3, s_res3 = s_sum.again(G * EU), s_fct.again(EU + 1), s_bd.again(EU + 1)
        s_outfix = sem("out_fix")

        block = ctx.enter_context(nc.Block())

        def node_rows(t, u):
            if u.j is None and u.c == NU - 1:
                return t[LAST:N, :].rearrange("(p g) d -> p g d", g=G)
            full = t[0:(NU - 1) * P * G, :].rearrange("(u p g) d -> u p g d", p=P, g=G)
            return full[u.times(1)]

        def edge_rows(t, u, width=D):
            if u.j is None and u.c == EU:
                return t[FIX:FIX + P, :].rearrange("(p g) d -> p g d", g=1)
            v = t[0:ES, :].rearrange("(p t) d -> p t d", p=P)
            return v[:, bass.ds(u.times(G), G), :]

        @block.sync
        def _(sp):
            sp.wait_ge(s_zero.sem, 1)
            sp.dma_start(dst_sorted[:, 1:1 + E], dst.rearrange("(a e) -> a e", a=1)).then_inc(s_staged.sem, 16)
            sp.dma_start(src_sorted[:, 0:E], src.rearrange("(a e) -> a e", a=1)).then_inc(s_staged.sem, 16)
            sp.dma_start(attr_sorted[0:E, :], edge_attr).then_inc(s_staged.sem, 16)
            sp.dma_start(dst_sorted[:, 0:1], pads[:, 0, 0:1]).then_inc(s_staged.sem, 16)
            sp.dma_start(dst_sorted[:, ES + 1:ES + 2], pads[:, 0, 1:2]).then_inc(s_staged.sem, 16)
            sp.dma_start(dst_sorted[:, 1 + E:1 + ES], pads[:, 1, 0:ES - E]).then_inc(s_staged.sem, 16)
            sp.dma_start(src_sorted[:, E:ES], pads[:, 2, 0:ES - E]).then_inc(s_staged.sem, 16)
            sp.dma_start(attr_sorted[E:ES, :], zeros[0:ES - E, 0:DE]).then_inc(s_staged.sem, 16)
            for k in range(2):
                sp.dma_start(node_tab[k * (N // 2):(k + 1) * (N // 2), :].rearrange(
                    "(p r) c -> p (r c)", p=FILL), fill[0:FILL, :]).then_inc(s_tab0.sem, 16)
            for t, v in ((w0[0:D, :], W0), (w0[D:DA, :], b0.rearrange("(a d) -> a d", a=1)),
                         (w1z[0:D, :], W1), (w1z[D:DA, :], b1.rearrange("(a d) -> a d", a=1)),
                         (w1g[D:DA, :], b1.rearrange("(a d) -> a d", a=1)),
                         (wa[0:D, 0:D], W_e[0:D, :]), (wa[0:D, D:2 * D], W_n[0:D, :]),
                         (wa[D:DA, 0:D], b_e.rearrange("(a d) -> a d", a=1)),
                         (wa[D:DA, D:2 * D], b_n.rearrange("(a d) -> a d", a=1)),
                         (wb[:, 0:D], W_e[D:2 * D, :]), (wb[:, D:2 * D], W_n[D:2 * D, :]),
                         (wc[:, 0:D], W_e[2 * D:, :]), (wc[:, D:2 * D], W_n[2 * D:, :]),
                         (g0c[:, :], g0.rearrange("(d a) -> d a", a=1)),
                         (g0b[:, :], g0.partition_broadcast(P)), (be0b[:, :], be0.partition_broadcast(P)),
                         (g1b[:, :], g1.partition_broadcast(P)), (be1b[:, :], be1.partition_broadcast(P))):
                sp.dma_start(t, v).then_inc(s_w.sem, 16)
            sp.wait_ge(s_const.sem, 1)
            sp.dma_start(pick[:, D:DA], be0.rearrange("(d a) -> d a", a=1)).then_inc(s_wz.sem, 16)
            sp.wait_ge(s_staged.sem, 16 * 8)
            for k in range(3):
                o = (1, 0, 2)[k]
                sp.dma_start(di[:, k, :], dst_sorted[0, o:o + ES].rearrange("(p t) -> p t", p=P)
                             ).then_inc(s_edges.sem, 16)
            sp.dma_start(si[:, :], src_sorted[0, :].rearrange("(p t) -> p t", p=P)).then_inc(s_edges.sem, 16)

            sp.wait_ge(s_order.sem, 1)
            unsorted = sp.value_load(falls[0:1, 0:1])
            with sp.If(unsorted > 0):
                sp.dma_start(attr_given, attr_sorted).then_inc(s_given.sem, 16)
                of_partition = dst_sorted[0, 1:1 + ES].rearrange("(p t) -> p t", p=P)
                sp.dma_start(others_i, of_partition[0].partition_broadcast(P)).then_inc(s_others.sem, 16)
                with sp.Fori(1, P) as c:
                    sp.wait_ge(s_others_used.sem, c * 1)
                    sp.dma_start(others_i, of_partition[c].partition_broadcast(P)).then_inc(s_others.sem, 16)
                sp.wait_ge(s_given.sem, 16)
                given = attr_given[:, :].rearrange("(p t) d -> p t d", p=P)
                sp.dma_start(edge.h[:, 0, :, 0:DE], given[:, 0:G, :]).then_inc(s_rows_in.sem, 16)
                with sp.Fori(1, EU) as j:
                    sp.wait_ge(s_resorted.sem, j * (16 * 3 * G))
                    sp.dma_start(edge.h[:, 0, :, 0:DE], given[:, bass.ds(j * G, G), :]
                                 ).then_inc(s_rows_in.sem, 16)
                sp.wait_ge(s_resorted.sem, EU * 16 * 3 * G)
                for k in range(3):
                    o = (1, 0, 2)[k]
                    sp.dma_start(di[:, k, :], dst_sorted[0, o:o + ES].rearrange("(p t) -> p t", p=P)
                                 ).then_inc(s_reloaded.sem, 16)
                sp.dma_start(si[:, :], src_sorted[0, :].rearrange("(p t) -> p t", p=P)
                             ).then_inc(s_reloaded.sem, 16)

            def load_node(u):
                if u.within(NU):
                    if (u - 4).exists:
                        sp.wait_ge(node.s_x1.sem, node.s_x1.upto(u - 4))
                    sp.dma_start(node.x[:, u.slot], node_rows(x, u)).then_inc(node.loaded[u.slot], 16)

            def store_node(u):
                if u.within(NU):
                    sp.wait_ge(node.s_o.sem, node.s_o.upto(u))
                    if u.j is None and u.c == NU - 1:
                        for slot in range(R):
                            sp.wait_ge(node.o_stored[slot], node.o_stored.all(slot, NU - 1))
                    sp.dma_start(node_rows(out, u), node.o[:, u.slot]).then_inc(node.o_stored[u.slot], 16)

            def store(table, tile, sems, u, last, ready, per=1):
                if u.within(last):
                    sp.wait_ge(ready.sem, ready.upto(u, per))
                    fix = u.j is None and u.c == EU
                    sp.dma_start(edge_rows(table, u), tile[:, u.slot, 0:1 if fix else G, :]
                                 ).then_inc(sems[u.slot], 16)

            def load2(u):
                if u.within(EU + 1):
                    fix = u.j is None and u.c == EU
                    n = 1 if fix else G
                    if u.j is None and u.c == 0:
                        for slot in range(R):
                            sp.wait_ge(zs_stored[slot], zs_stored.all(slot, EU))
                        for slot in range(R):
                            sp.wait_ge(xd_stored[slot], xd_stored.all(slot, EU + 1))
                        for slot in range(R):
                            sp.wait_ge(zd_stored[slot], zd_stored.all(slot, EU + 1))
                    if (u - R).exists:
                        sp.wait_ge(e2.s_u.sem, e2.s_u.upto(u - R))
                    if not fix:
                        sp.dma_start(zs2[:, u.slot], edge_rows(z_src, u)).then_inc(zs2_loaded[u.slot], 16)
                    sp.dma_start(zd2[:, u.slot, 0:n, :], edge_rows(z_dst, u)).then_inc(zd2_loaded[u.slot], 16)
                    if (u - 4).exists:
                        sp.wait_ge(e2.s_x1.sem, e2.s_x1.upto(u - 4))
                    sp.dma_start(e2.x[:, u.slot, 0:n, :], edge_rows(x_dst, u)).then_inc(e2.loaded[u.slot], 16)

            load_node(At(None, 0))

            def step(s):
                load_node(s + 1)
                a, b = s - S1, s - S2
                store_node(s - 5)
                store(sum_tab[0], sums, sum_stored, a, EU, s_sum, G)
                store(x_dst, xd, xd_stored, a, EU + 1, s_bd)
                store(z_src, zs, zs_stored, a - 2, EU, s_zs)
                store(z_dst, zd, zd_stored, a - 2, EU + 1, s_zd)
                load2(b + 1)
                store(h_src, edge.h, hs_stored, a - 4, EU, edge.s_h)
                store(sum_tab[1], sums2, sum2_stored, b, EU, s_sum2, G)
                store(h_dst, e2.h, hd_stored, b - 3, EU + 1, e2.s_h)
                store(o_dst, e2.o, e2.o_stored, b - 4, EU + 1, e2.s_o)

            run_steps(sp, step)

            for slot in range(R):
                sp.wait_ge(hs_stored[slot], hs_stored.all(slot, EU))
            for slot in range(R):
                sp.wait_ge(hd_stored[slot], hd_stored.all(slot, EU + 1))
            for slot in range(R):
                sp.wait_ge(e2.o_stored[slot], e2.o_stored.all(slot, EU + 1))

            def load3(u):
                if u.within(EU + 1):
                    fix = u.j is None and u.c == EU
                    if (u - 4).exists:
                        sp.wait_ge(s_res3.sem, s_res3.upto(u - 4))
                    if not fix:
                        sp.dma_start(hs3[:, u.slot, :, 0:D], edge_rows(h_src, u)).then_inc(hs3_loaded[u.slot], 16)
                        sp.dma_start(at3[:, u.slot], edge_rows(attr_sorted, u)).then_inc(rest3_loaded[u.slot], 16)
                    sp.dma_start(o3[:, u.slot, 0:1 if fix else G, :], edge_rows(o_dst, u)
                                 ).then_inc(rest3_loaded[u.slot], 16)

            load3(At(None, 0))
            load3(At(None, 1))
            load3(At(None, 2))

            def step3(s):
                load3(s + 3)
                store(sum_tab[2], sums3, sum3_stored, s, EU, s_sum3, G)

            run_steps(sp, step3, SEGMENTS3)
            for slot in range(R):
                sp.wait_ge(node.o_stored[slot], node.o_stored.all(slot, NU))

        @block.gpsimd
        def _(pool):
            pool.memset(ident[:], 0.0).then_inc(s_ident.sem, 1)
            pool.wait_ge(s_ident.sem, 1)
            pool.affine_select(out=ident[:], in_=ident[:], compare_op=ALU.not_equal, fill=1.0, base=0,
                               pattern=[[-1, P]], channel_multiplier=1).then_inc(s_ident.sem, 1)
            pool.iota(iota_i[:], pattern=[[1, T]], base=0, channel_multiplier=0).then_inc(s_ident.sem, 1)
            pool.iota(part_i[:], pattern=[[1, P]], base=0, channel_multiplier=0).then_inc(s_ident.sem, 1)
            pool.iota(idx_fix[:, 3:4], pattern=[[0, 1]], base=0, channel_multiplier=1).then_inc(s_ident.sem, 1)

            def rstd(c, b, u, sets):
                w = u.c % 2
                pool.wait_ge(c.s_var[b].sem, c.s_var[b].upto(u))
                pool.tensor_tensor(c.rstd[b][:, w, 0:sets], c.var[b][:, w, 0:sets], mhalf[:, 0:sets],
                                   ALU.pow).then_inc(c.s_rstd[b].sem, 1)

            def gather(to, table, index, bound, landed_):
                pool.indirect_dma_start(out=to, out_offset=None, in_=table,
                                        in_offset=bass.IndirectOffsetOnAxis(ap=index, axis=0),
                                        bounds_check=bound, oob_is_err=False).then_inc(landed_, 16)

            def scatter(table, index, rows, bound, landed_):
                pool.indirect_dma_start(out=table, out_offset=bass.IndirectOffsetOnAxis(ap=index, axis=0),
                                        in_=rows, in_offset=None,
                                        bounds_check=bound, oob_is_err=False).then_inc(landed_, 16)

            pool.memset(idle[:], 0.0).then_inc(s_ident.sem, 1)
            pool.wait_ge(s_ident.sem, 6)

            def before_dmas(k, u):
                if u.number is None:
                    pool.tensor_tensor(idle[:, 1, k, u.slot:u.slot + 1], idle[:, 0, k, u.slot:u.slot + 1],
                                       idle[:, 0, k, u.slot:u.slot + 1], ALU.add)

            pool.wait_ge(s_order.sem, 1)
            unsorted = pool.value_load(falls[0:1, 0:1])
            with pool.If(unsorted > 0):
                pool.wait_ge(s_rank.sem, RANKED)
                with pool.Fori(0, EU) as j:
                    pool.wait_ge(s_rows_in.sem, j * 16 + 16)
                    now = bass.ds(j * G, G)
                    pool.tensor_copy(ixr[:, 0, :, 0], rank_i[:, 0, now]).then_inc(s_sort_copied.sem, 1)
                    pool.tensor_copy(ixr[:, 0, :, 1], rank_i[:, 1, now]).then_inc(s_sort_copied.sem, 1)
                    pool.tensor_copy(ixr[:, 0, :, 2], di[:, 0, now]).then_inc(s_sort_copied.sem, 1)
                    pool.tensor_copy(ixr[:, 0, :, 3], si[:, now]).then_inc(s_sort_copied.sem, 1)
                    pool.wait_ge(s_sort_copied.sem, j * 4 + 4)
                    pool.tensor_tensor(idle[:, 1, 5, 0:1], idle[:, 0, 5, 0:1], idle[:, 0, 5, 0:1], ALU.add)
                    for g in range(G):
                        scatter(dst_sorted.rearrange("a (e b) -> (a e) b", b=1), ixr[:, 0, g, 1:2], ixr[:, 0, g, 2:3],
                                ES, s_resorted.sem)
                        scatter(src_sorted.rearrange("a (e b) -> (a e) b", b=1), ixr[:, 0, g, 0:1], ixr[:, 0, g, 3:4],
                                ES - 1, s_resorted.sem)
                        scatter(attr_sorted, ixr[:, 0, g, 0:1], edge.h[:, 0, g, 0:DE], ES - 1, s_resorted.sem)
                    pool.wait_ge(s_resorted.sem, j * (16 * 3 * G) + 16 * 3 * G)
                    pool.tensor_tensor(idle[:, 1, 5, 1:2], idle[:, 0, 5, 1:2], idle[:, 0, 5, 1:2], ALU.add)

            def put_tab(u):
                if not u.within(EU):
                    return
                if (u - R).exists:
                    pool.wait_ge(s_put[(u - R).slot], s_put.upto(u - R, 16 * G))
                pool.tensor_copy(ixr[:, u.slot, :, 4], idx[:, bass.ds(u.times(G), G), 4]).then_inc(s_copied.sem, 1)
                pool.tensor_copy(payr[:, u.slot], pay[:, bass.ds(u.times(G), G), :]).then_inc(s_copied.sem, 1)
                pool.wait_ge(s_copied.sem, s_copied.upto(u, 2))
                before_dmas(0, u)
                for g in range(G):
                    scatter(node_tab, ixr[:, u.slot, g, 4:5], payr[:, u.slot, g, :], N - 1, s_put[u.slot])

            def take_tab(u):
                if u.within(EU + R, R):
                    v = u - R
                    pool.wait_ge(s_got[v.slot], s_got.upto(v, 16 * G))
                    pool.tensor_copy(seen[:, bass.ds(v.times(G), G), :], seenr[:, v.slot]).then_inc(s_seen.sem, 1)
                if not u.within(EU):
                    return
                pool.tensor_copy(ixr[:, u.slot, :, 0], idx[:, bass.ds(u.times(G), G), 0]).then_inc(s_copied.sem, 1)
                pool.wait_ge(s_copied.sem, u.times(1, 2 * EU + 1))
                if u.number is None or u.number >= R:
                    pool.wait_ge(s_seen.sem, u.times(1, 1 - R))
                before_dmas(1, u)
                for g in range(G):
                    gather(seenr[:, u.slot, g, :], node_tab, ixr[:, u.slot, g, 0:1], N - 1, s_got[u.slot])

            def gather_sources(u):
                if not u.within(EU):
                    return
                if (u - R).exists:
                    pool.wait_ge(edge.loaded[(u - R).slot], edge.loaded.upto(u - R, 16 * G))
                if (u - R).exists:
                    pool.wait_ge(xd_loaded[(u - R).slot], xd_loaded.upto(u - R, 16 * G))
                pool.tensor_copy(ixr[:, u.slot], idx[:, bass.ds(u.times(G), G), :]).then_inc(s_ix1.sem, 1)
                pool.wait_ge(s_ix1.sem, s_ix1.upto(u))
                if (u - R).exists:
                    pool.wait_ge(edge.s_x1.sem, edge.s_x1.upto(u - R))
                before_dmas(2, u)
                for g in range(G):
                    gather(edge.x[:, u.slot, g, :], x, ixr[:, u.slot, g, 0:1], N - 1, edge.loaded[u.slot])

            def gather_dests(u):
                if not u.within(EU + 1):
                    return
                if (u - R).exists:
                    pool.wait_ge(xd_stored[(u - R).slot], xd_stored.upto(u - R))
                if (u - R).exists:
                    pool.wait_ge(s_bd.sem, s_bd.upto(u - R))
                if u.number == EU:
                    gather(xd[:, u.slot, 0, :], x, idx_fix[:, 0:1], N - 1, xd_loaded[u.slot])
                    return
                before_dmas(3, u)
                for g in range(G):
                    gather(xd[:, u.slot, g, :], x, ixr[:, u.slot, g, 1:2], N - 1, xd_loaded[u.slot])

            def gather_ends(k, stored):
                for slot in range(R):
                    pool.wait_ge(stored[slot], stored.all(slot, EU))
                gather(ends[:, k, :], sum_tab[k], idx_fix[:, 2:3], ES - 1, s_ends.sem)

            def lay2(u):
                if not u.within(EU):
                    return
                if (u - R).exists:
                    pool.wait_ge(zs2_laid[(u - R).slot], zs2_laid.upto(u - R, 16 * G))
                pool.tensor_copy(ixr3[:, u.slot], idx[:, bass.ds(u.times(G), G), :]).then_inc(s_ix2.sem, 1)
                pool.wait_ge(s_ix2.sem, s_ix2.upto(u))
                pool.wait_ge(zs2_loaded[u.slot], zs2_loaded.upto(u))
                before_dmas(4, u)
                for g in range(G):
                    gather(zs2[:, u.slot, g, :], z_dst, ixr3[:, u.slot, g, 2:3], ROWS - 1, zs2_laid[u.slot])

            def step(s):
                a, b = s - S1, s - S2
                if s.number == PUT:
                    pool.wait_ge(s_idx.sem, 1)
                    pool.wait_ge(s_tab0.sem, 32)
                    scatter(node_tab, idx_fix[:, 1:2], pay_fix[:, :], N - 1, s_putfix.sem)
                if s.number == TAKE:
                    for slot in range(R):
                        pool.wait_ge(s_put[slot], s_put.all(slot, EU, 16 * G))
                    pool.wait_ge(s_putfix.sem, 16)
                if a.number == EU:
                    gather_ends(0, sum_stored)
                if b.number == EU:
                    gather_ends(1, sum2_stored)
                if s.number == S2 - 1:
                    for slot in range(R):
                        pool.wait_ge(zd_stored[slot], zd_stored.all(slot, EU + 1))
                if s.within(NU + 3):
                    rstd(node, 0, s, 2 * G)
                if s.within(NU + 2):
                    rstd(node, 1, s, 2 * G)
                if a.within(EU + 3):
                    rstd(edge, 0, a, 3 * G)
                if a.within(EU + 2):
                    rstd(edge, 1, a, 3 * G)
                if b.within(EU + 3, 1):
                    rstd(e2, 0, b - 1, 2 * G)
                put_tab(s - PUT)
                take_tab(s - TAKE)
                if s.number == S1 - 1:
                    pool.wait_ge(s_fac.sem, 1)
                gather_sources(a + 1)
                gather_dests(a + 1)
                lay2(b + 1)

            run_steps(pool, step)

            def gather3(u):
                if not u.within(EU):
                    return
                if (u - R).exists:
                    pool.wait_ge(hs3_laid[(u - R).slot], hs3_laid.upto(u - R, 16 * G))
                if (u - R).exists:
                    pool.wait_ge(hd3_got[(u - R).slot], hd3_got.upto(u - R, 16 * G))
                pool.tensor_copy(ixr[:, u.slot], idx[:, bass.ds(u.times(G), G), :]).then_inc(s_ix3.sem, 1)
                pool.wait_ge(s_ix3.sem, s_ix3.upto(u))
                if (u - R).exists:
                    pool.wait_ge(s_tp3.sem, s_tp3.upto(u - R))
                before_dmas(6, u)
                for g in range(G):
                    gather(hd3[:, u.slot, g, :], h_dst, ixr[:, u.slot, g, 3:4], ROWS - 1, hd3_got[u.slot])
                pool.wait_ge(hs3_loaded[u.slot], hs3_loaded.upto(u))
                before_dmas(5, u)
                for g in range(G):
                    gather(hs3[:, u.slot, g, 0:D], h_dst, ixr[:, u.slot, g, 2:3], ROWS - 1, hs3_laid[u.slot])

            def put3(u):
                if u.number == EU:
                    pool.wait_ge(s_res3.sem, s_res3.upto(u))
                    scatter(out, idx_fix[:, 1:2], res3[:, u.slot, 0, :], N - 1, s_outfix.sem)
                if not u.within(EU):
                    return
                if (u - R).exists:
                    pool.wait_ge(out_put[(u - R).slot], out_put.upto(u - R, 16 * G))
                pool.tensor_copy(ixr3[:, u.slot, :, 4], idx[:, bass.ds(u.times(G), G), 4]).then_inc(s_ixput3.sem, 1)
                pool.wait_ge(s_ixput3.sem, s_ixput3.upto(u))
                pool.wait_ge(s_res3.sem, s_res3.upto(u))
                before_dmas(7, u)
                for g in range(G):
                    scatter(out, ixr3[:, u.slot, g, 4:5], res3[:, u.slot, g, :], N - 1, out_put[u.slot])

            for slot in range(R):
                pool.wait_ge(hd_stored[slot], hd_stored.all(slot, EU + 1))
            gather3(At(None, 0))

            def step3(s):
                if s.number == 0:
                    for slot in range(R):
                        pool.wait_ge(node.o_stored[slot], node.o_stored.all(slot, NU))
                gather3(s + 1)
                put3(s - 2)
                if s.number == EU:
                    gather_ends(2, sum3_stored)

            run_steps(pool, step3, SEGMENTS3)
            for slot in range(R):
                pool.wait_ge(out_put[slot], out_put.all(slot, EU, 16 * G))
            pool.wait_ge(s_outfix.sem, 16)

        @block.scalar
        def _(act):
            def copy_ut(k, n, before, ready, u):
                act.wait_ge(before.sem, before.upto(u))
                nc.scalar.copy(ut[0:n, k, :], TPS[k][0:n, :]).then_inc(ready.sem, 1)

            def tanh(to, k, scale, before, ready, u, n=G):
                act.wait_ge(before.sem, before.upto(u))
                for g in range(n):
                    i = nc.scalar.activation(to[:, g, :], qv(k, g), ACT.Tanh, scale=scale[:, g:g + 1])
                i.then_inc(ready.sem, 1)

            def relu_x1(c, k, first, u, t):
                act.wait_ge(c.s_nb.sem, c.s_nb.upto(u))
                for g in range(G):
                    i = nc.scalar.activation(c.h[:, u.slot, g, :], c.x1[:, u.slot, g, :], ACT.Relu,
                                             bias=c.nb[:, t.c % 2, g:g + 1],
                                             scale=c.rstd[k][:, t.c % 2, first + g:first + g + 1])
                i.then_inc(c.s_h.sem, 1)

            def chain(c, k, t, n):
                w = t.c % 2
                if t.within(n):
                    copy_ut(k, DA, c.s_tp1, c.s_ut1, t)
                if (t - 1).within(n):
                    copy_ut(k + 1, DA, c.s_tp2, c.s_ut2, t - 1)
                if c is edge and t.within(n + 1):
                    copy_ut(k, DA, s_udt, s_utd, t)
                if t.within(n):
                    tanh(c.a1[:, w, :, 0:D], k, c.rstd[0][:, w, 0:G], c.s_q1, c.s_a1, t)
                if (t - 1).within(n):
                    if (t - 3).exists:
                        act.wait_ge(c.s_x1.sem, c.s_x1.upto(t - 3))
                    tanh(c.a2[:, (t.c - 1) % 2], k + 1, c.rstd[1][:, w, 0:G], c.s_q2, c.s_a2, t - 1)
                if c is edge and t.within(n + 1):
                    m = 1 if t.number == n else G
                    if (t - 2).exists:
                        act.wait_ge(s_zd.sem, s_zd.upto(t - 2))
                    tanh(ad[:, w], k, fct[:, w, :, 1], s_qd, s_ad, t, m)
                if (t - 3).within(n):
                    if c is edge:
                        if (t - 3 - R).exists:
                            act.wait_ge(hs_stored[(t - 3 - R).slot], hs_stored.upto(t - 3 - R))
                    else:
                        if (t - 3 - R).exists:
                            act.wait_ge(c.s_o.sem, c.s_o.upto(t - 3 - R))
                    relu_x1(c, 0, G, t - 3, t)

            def chain2(t):
                if t.within(EU + 1):
                    w, m = t.c % 2, 1 if t.number == EU else G
                    copy_ut(2, DA, e2.s_tp1, e2.s_ut1, t)
                    if (t - 2).exists:
                        act.wait_ge(e2.s_x1.sem, e2.s_x1.upto(t - 2))
                    tanh(e2.a2[:, w], 2, fct2[:, w, :, 1], e2.s_q1, e2.s_a2, t, m)
                if (t - 2).within(EU + 1):
                    if (t - 2 - R).exists:
                        act.wait_ge(hd_stored[(t - 2 - R).slot], hd_stored.upto(t - 2 - R))
                    if (t - 2 - R).exists:
                        act.wait_ge(e2.s_o.sem, e2.s_o.upto(t - 2 - R))
                    relu_x1(e2, 0, G, t - 2, t - 1)

            def step(s):
                chain(node, 0, s, NU)
                chain(edge, 2, s - S1, EU)
                chain2(s - S2)

            run_steps(act, step)

            def copy_rows(u):
                act.wait_ge(s_tp3.sem, s_tp3.upto(u))
                if (u - 1).exists:
                    act.wait_ge(s_q3.sem, s_q3.upto(u - 1))
                nc.scalar.copy(ut[0:DA, 0, :], TPS[0][0:DA, :]).then_inc(s_ut3.sem, 1)
                nc.scalar.copy(ut[0:D, 1, :], TPS[1][0:D, :]).then_inc(s_ut3.sem, 1)

            def step3(u):
                if not u.within(EU):
                    return
                if u.number == 0:
                    copy_rows(u)
                act.wait_ge(s_q3.sem, s_q3.upto(u))
                q = QALL[:, 1024 * (u.c % 2):1024 * (u.c % 2) + 1024].rearrange(
                    "p (b f) -> p b f", b=2)[:, :, 0:4 * D].rearrange("p b (g f) -> p b g f", g=2)
                if (u - 1).exists:
                    act.wait_ge(s_gt3.sem, s_gt3.upto(u - 1))
                for b in range(2):
                    i = nc.scalar.activation(eg3[:, 2 * b:2 * b + 2, :], q[:, b, :, 0:D], ACT.Exp, scale=-1.0)
                i.then_inc(s_exp3.sem, 1)
                for b in range(2):
                    i = nc.scalar.activation(ab3[:, 2 * b:2 * b + 2, :], q[:, b, :, D:2 * D], ACT.Abs)
                i.then_inc(s_abs3.sem, 1)
                act.wait_ge(s_abs3.sem, s_abs3.upto(u))
                nc.scalar.activation(ex3[:], ab3[:], ACT.Exp, scale=-1.0).then_inc(s_ea3.sem, 1)
                if (u + 1).within(EU):
                    copy_rows(u + 1)
                act.wait_ge(s_ea3.sem, s_ea3.upto(u))
                nc.scalar.activation(ln3[:], ex3[:], ACT.Ln, bias=1.0).then_inc(s_ln3.sem, 1)

            run_steps(act, step3, SEGMENTS3)

        @block.tensor
        def _(pe):
            def turn(rows, k, n, ready, m=G):
                for g in range(m):
                    i = pe.transpose(TPS[k][0:n, g * P:(g + 1) * P], rows[:, g, :], ident[:, :])
                i.then_inc(ready.sem, 1)

            def product(k, w, ready, m=G):
                for g in range(m):
                    i = pe.matmul(qv(k, g), ut[:, k, g * P:(g + 1) * P], w[:, :], start=True, stop=True)
                i.then_inc(ready.sem, 1)

            def fix_total(k, last):
                pe.wait_ge(s_ends.sem, 16 * (k + 1))
                out_ = QS[3][:, 4 * D:5 * D]
                pe.matmul(out_, eq_ff[:, :], ends[:, k, :], start=True, stop=False)
                pe.matmul(out_, eq_lf[:, :], last, start=False, stop=True).then_inc(s_tot.sem, 1)

            pe.wait_ge(s_ident.sem, 2)
            pe.wait_ge(s_w1in.sem, 1)
            pe.wait_ge(s_wz.sem, 16)
            pe.matmul(QS[0][0:DA, 0:D], centre[:, :], w1g[0:D, :], start=True, stop=False)
            pe.matmul(QS[0][0:DA, 0:D], pick[:, :], w1z[0:D, :], start=False, stop=True).then_inc(s_wmm.sem, 1)
            pe.wait_ge(s_falls.sem, 1)
            pe.matmul(QS[2][0:1, 0:1], cols[:, 7:8], hs3[:, 0, 0, D:DA], start=True, stop=True
                      ).then_inc(s_falls_sum.sem, 1)
            pe.wait_ge(s_rowin.sem, 1)
            pe.transpose(TPS[0][:, 0:P], firsts[:, :], ident[:, :]).then_inc(s_row.sem, 1)
            pe.wait_ge(s_cntin.sem, 1)
            pe.matmul(QS[1][:, 0:1], eq_ff[:, :], ends_cnt[:, 0:1], start=True, stop=False)
            pe.matmul(QS[1][:, 0:1], eq_lf[:, :], ends_cnt[:, 1:2], start=False, stop=True).then_inc(s_cnt.sem, 1)
            pe.wait_ge(s_w1n.sem, 1)
            pe.wait_ge(s_idx.sem, 1)

            def chain(c, k, t, n):
                w = t.c % 2
                if t.within(n):
                    pe.wait_ge(c.s_u.sem, c.s_u.upto(t))
                    turn(c.u[:, w], k, DA, c.s_tp1)
                if (t - 1).within(n):
                    pe.wait_ge(c.s_a1_std.sem, c.s_a1_std.upto(t - 1))
                    turn(c.a1[:, (t.c - 1) % 2], k + 1, DA, c.s_tp2)
                if t.within(n):
                    pe.wait_ge(c.s_ut1.sem, c.s_ut1.upto(t))
                    if c is edge:
                        if (t - 1).exists:
                            pe.wait_ge(s_ad.sem, s_ad.upto(t - 1))
                    else:
                        if (t - 1).exists:
                            pe.wait_ge(c.s_a1.sem, c.s_a1.upto(t - 1))
                    product(k, w0, c.s_q1)
                if c is edge and t.within(n + 1):
                    m = 1 if t.number == n else G
                    pe.wait_ge(s_bd.sem, s_bd.upto(t))
                    turn(bd[:, w], k, DA, s_udt, m)
                if (t - 1).within(n):
                    pe.wait_ge(c.s_ut2.sem, c.s_ut2.upto(t - 1))
                    if (t - 2).exists:
                        pe.wait_ge(c.s_a2.sem, c.s_a2.upto(t - 2))
                    product(k + 1, w1n, c.s_q2)
                if c is edge and t.within(n + 1):
                    pe.wait_ge(s_utd.sem, s_utd.upto(t))
                    if (t - 1 if t.number == n else t).exists:
                        pe.wait_ge(c.s_a1.sem, c.s_a1.upto(t - 1 if t.number == n else t))
                    product(k, w0, s_qd, m)

            def step(s):
                chain(node, 0, s, NU)
                a, t = s - S1, s - S2
                if a.number == EU:
                    fix_total(0, sums[:, (EU - 1) % R, G - 1, :])
                chain(edge, 2, a, EU)
                if t.number == EU:
                    fix_total(1, sums2[:, (EU - 1) % R, G - 1, :])
                if t.within(EU + 1):
                    m = 1 if t.number == EU else G
                    pe.wait_ge(e2.s_u.sem, e2.s_u.upto(t))
                    turn(e2.u[:, t.c % 2], 2, DA, e2.s_tp1, m)
                    pe.wait_ge(e2.s_ut1.sem, e2.s_ut1.upto(t))
                    if (t - 1).exists:
                        pe.wait_ge(e2.s_a2.sem, e2.s_a2.upto(t - 1))
                    product(2, w1z, e2.s_q1, m)

            run_steps(pe, step)

            def step3(u):
                if u.number == EU:
                    fix_total(2, sums3[:, (EU - 1) % R, G - 1, :])
                if not u.within(EU):
                    return
                pe.wait_ge(rest3_loaded[u.slot], rest3_loaded.upto(u, 32))
                pe.wait_ge(hd3_got[u.slot], hd3_got.upto(u, 16 * G))
                pe.wait_ge(hs3_laid[u.slot], hs3_laid.upto(u, 16 * G))
                if (u - 1).exists:
                    pe.wait_ge(s_ut3.sem, s_ut3.upto(u - 1, 3))
                for g in range(G):
                    c = slice(g * P, (g + 1) * P)
                    pe.transpose(TPS[0][0:DA, c], hs3[:, u.slot, g, :], ident[:, :])
                    pe.transpose(TPS[1][0:D, c], hd3[:, u.slot, g, :], ident[:, :])
                    i = pe.transpose(TPS[2][0:DE, c], at3[:, u.slot, g, :], ident[:, :])
                i.then_inc(s_tp3.sem, 1)
                pe.wait_ge(s_ut3.sem, s_ut3.upto(u, 3))
                if (u - 2).exists:
                    pe.wait_ge(s_gt3.sem, s_gt3.upto(u - 2))
                for g in range(G):
                    c = slice(g * P, (g + 1) * P)
                    q = 1024 * (u.c % 2) + 512 * (g // 2) + 2 * D * (g % 2)
                    o = QALL[:, q:q + 2 * D]
                    pe.matmul(o, ut[0:DA, 0, c], wa[:, :], start=True, stop=False)
                    pe.matmul(o, ut[0:D, 1, c], wb[:, :], start=False, stop=False)
                    i = pe.matmul(o, ut[0:DE, 2, c], wc[:, :], start=False, stop=True)
                i.then_inc(s_q3.sem, 1)

            run_steps(pe, step3, SEGMENTS3)

        @block.vector
        def _(dve):
            order = count(1)

            for t, v in ((mhalf, -0.5), (zeros, 0.0), (centre[:, 0:D], -1.0 / D), (centre[:, D:DA], 0.0),
                         (pick[:, 0:D], 0.0), (hs3[:, :, :, D], 1.0), (pads[:, 0, 0:1], -1),
                         (pads[:, 0, 1:2], N + 1), (pads[:, 1, :], N), (pads[:, 2, :], 0)):
                dve.memset(t if isinstance(t, bass.AP) else t[:], v)
            f = fill[:, :].rearrange("p (r c) -> p r c", c=2)
            dve.memset(f[:, :, 0], float(SKIP))
            dve.memset(f[:, :, 1], 0.0)
            for c in (node, edge, e2):
                for b in c.bn:
                    dve.memset(b[:], 1.0)
            dve.memset(tmpa[:], 0.0).then_inc(s_prep.sem, 1)
            dve.wait_ge(s_prep.sem, next(order))
            dve.memset(cols[:], 0.0).then_inc(s_zero.sem, 1)
            dve.memset(dis[:, 0:1], 0.0).then_inc(s_const.sem, 1)
            dve.wait_ge(s_w.sem, 16 * 18)
            dve.tensor_scalar(w1g[0:D, :], w1z[0:D, :], g0c[:, 0:1], None, ALU.mult).then_inc(s_w1in.sem, 1)
            dve.wait_ge(s_wmm.sem, 1)
            dve.wait_ge(s_w1in.sem, 1)
            dve.tensor_tensor(w1n[:, :], QS[0][0:DA, 0:D], w1g[:, :], ALU.add).then_inc(s_w1n.sem, 1)

            dve.wait_ge(s_edges.sem, 16 * 4)
            dve.wait_ge(s_ident.sem, 5)
            dve.tensor_copy(df[:], di[:])
            dve.tensor_copy(col[:], iota_i[:])
            dve.tensor_copy(cols[:, 8:9], idx_fix[:, 3:4]).then_inc(s_prep.sem, 1)
            dve.wait_ge(s_prep.sem, next(order))
            own, before, after = df[:, 0, :], df[:, 1, :], df[:, 2, :]
            dve.tensor_tensor(tmpa[:], own, after, ALU.is_gt).then_inc(s_prep.sem, 1)
            dve.wait_ge(s_prep.sem, next(order))
            dve.tensor_reduce(cols[:, 7:8], tmpa[:], AX.X, ALU.max).then_inc(s_falls.sem, 1)
            dve.wait_ge(s_falls_sum.sem, 1)
            dve.tensor_copy(falls[:, :], QS[2][0:1, 0:1]).then_inc(s_order.sem, 1)
            dve.wait_ge(s_order.sem, 1)
            unsorted = dve.value_load(falls[0:1, 0:1])
            with dve.If(unsorted > 0):
                dve.memset(rank_f, 0.0)
                dve.tensor_copy(others_no, col[:])
                dve.tensor_scalar(cols[:, 9:10], cols[:, 8:9], float(T), None, ALU.mult).then_inc(s_rank.sem, 1)
                dve.wait_ge(s_rank.sem, 1)
                dve.tensor_scalar(own_no, col[:], cols[:, 9:10], None, ALU.add).then_inc(s_rank.sem, 1)
                dve.wait_ge(s_rank.sem, 2)
                with dve.Fori(0, P) as c:
                    per = 5 * (T // 7) + 2
                    dve.wait_ge(s_others.sem, c * 16 + 16)
                    dve.tensor_copy(others_f, others_i).then_inc(s_rank.sem, 1)
                    dve.wait_ge(s_rank.sem, c * per + 3)
                    dve.memset(zt[:, 0, 1, 0:1], 0.0)
                    with dve.Fori(0, T // 7) as j:
                        now = bass.ds(j * 7, 7)
                        lower, moved, less = own_t
                        at = c * per + j * 5 + 3

                        def of_all(row):
                            return row.unsqueeze(1).broadcast_to([P, 7, T])

                        def of_own(row):
                            return row[:, now].unsqueeze(2).broadcast_to([P, 7, T])

                        dve.tensor_tensor(lower, of_all(others_no), of_own(own_no), ALU.is_lt
                                          ).then_inc(s_rank.sem, 1)
                        dve.wait_ge(s_rank.sem, at + 1)
                        dve.scalar_tensor_tensor(out=moved, in0=lower, scalar=-0.5, in1=of_all(others_f),
                                                 op0=ALU.mult, op1=ALU.add).then_inc(s_rank.sem, 1)
                        dve.wait_ge(s_rank.sem, at + 2)
                        dve.tensor_tensor(less, moved, of_own(own), ALU.is_lt).then_inc(s_rank.sem, 1)
                        dve.wait_ge(s_rank.sem, at + 3)
                        dve.tensor_reduce(zt[:, 0, 0, 0:7], less, AX.X, ALU.add).then_inc(s_rank.sem, 1)
                        dve.wait_ge(s_rank.sem, at + 4)
                        dve.tensor_tensor(rank_f[:, now], rank_f[:, now], zt[:, 0, 0, 0:7], ALU.add
                                          ).then_inc(s_rank.sem, 1)
                        dve.wait_ge(s_rank.sem, at + 5)
                        dve.memset(zt[:, 0, 1, 0:1], 0.0)
                    dve.tensor_scalar(others_no, others_no, float(T), None, ALU.add).then_inc(s_rank.sem, 1)
                    dve.wait_ge(s_rank.sem, c * per + (2 + per))
                    dve.memset(zt[:, 0, 1, 0:1], 0.0).then_inc(s_others_used.sem, 1)
                dve.tensor_copy(rank_i[:, 0, :], rank_f)
                dve.tensor_scalar(rank_i[:, 1, :], rank_f, 1.0, None, ALU.add).then_inc(s_rank.sem, 1)
                dve.wait_ge(s_reloaded.sem, 16 * 4)
                dve.tensor_copy(df[:], di[:]).then_inc(s_rank.sem, 1)
                dve.wait_ge(s_rank.sem, RANKED + 1)

            dve.tensor_copy(part[:], part_i[:])
            first, last_ = df[:, 0, 0:1], df[:, 0, T - 1:T]
            dve.tensor_copy(firsts[:], first.broadcast_to([P, P])).then_inc(s_rowin.sem, 1)
            dve.tensor_tensor(same[:], own, before, ALU.is_equal)
            dve.tensor_tensor(tmpa[:], own, after, ALU.is_equal)
            dve.tensor_scalar(in_first[:], own, first, None, ALU.is_equal)
            dve.tensor_scalar(in_last[:], own, last_, None, ALU.is_equal)
            dve.tensor_tensor(cols[:, 2:3], first, last_, ALU.not_equal)
            dve.tensor_tensor(cols[:, 3:4], df[:, 2, T - 1:T], first, ALU.not_equal).then_inc(s_prep.sem, 1)
            dve.wait_ge(s_prep.sem, next(order))
            dve.tensor_reduce(ends_cnt[:, 0:1], in_first[:], AX.X, ALU.add)
            dve.tensor_reduce(ends_cnt[:, 1:2], in_last[:], AX.X, ALU.add)
            dve.tensor_copy(cols[:, 0:1], same[:, 0:1])
            dve.tensor_copy(cols[:, 1:2], tmpa[:, T - 1:T])
            dve.tensor_scalar(rep[:], tmpa[:], -1.0, 1.0, ALU.mult, ALU.add).then_inc(s_prep.sem, 1)
            dve.wait_ge(s_prep.sem, next(order))
            dve.memset(same[:, 0:1], 0.0)
            dve.tensor_scalar(in_first[:], in_first[:], cols[:, 0:1], None, ALU.mult)
            dve.tensor_scalar(in_last[:], in_last[:], cols[:, 1:2], None, ALU.mult)
            dve.tensor_tensor(cols[:, 4:5], cols[:, 0:1], cols[:, 3:4], ALU.mult).then_inc(s_prep.sem, 1)
            dve.wait_ge(s_prep.sem, next(order))
            dve.tensor_scalar(scan[:, 0, :], same[:], -1.0, 1.0, ALU.mult, ALU.add)
            dve.tensor_scalar(scanb[:, 0, :], in_first[:], -1.0, 1.0, ALU.mult, ALU.add)
            dve.scalar_tensor_tensor(out=scan[:, 1, :], in0=tmpa[:], scalar=1024.0, in1=col[:],
                                     op0=ALU.mult, op1=ALU.add).then_inc(s_prep.sem, 1)
            dve.wait_ge(s_prep.sem, next(order))
            dve.memset(scan[:, 1, T - 1:T], float(T - 1))
            dve.tensor_tensor(rep[:], rep[:], scanb[:, 0, :], ALU.mult)
            dve.tensor_tensor(scan[:, 0, :], scan[:, 0, :], col[:], ALU.mult).then_inc(s_prep.sem, 1)
            dve.wait_ge(s_prep.sem, next(order))
            k, a, b = 1, scan, scanb
            while k < T:
                dve.tensor_copy(b[:, 0, 0:k], a[:, 0, 0:k])
                dve.tensor_tensor(b[:, 0, k:T], a[:, 0, k:T], a[:, 0, 0:T - k], ALU.max)
                dve.tensor_copy(b[:, 1, T - k:T], a[:, 1, T - k:T])
                dve.tensor_tensor(b[:, 1, 0:T - k], a[:, 1, 0:T - k], a[:, 1, k:T], ALU.min).then_inc(s_prep.sem, 1)
                dve.wait_ge(s_prep.sem, next(order))
                k, a, b = 2 * k, b, a
            dve.tensor_tensor(tmpa[:], col[:], a[:, 0, :], ALU.subtract).then_inc(s_prep.sem, 1)
            dve.wait_ge(s_prep.sem, next(order))
            dve.tensor_scalar(pay[:, :, 1], tmpa[:], 1.0, None, ALU.add)
            dve.tensor_scalar(cols[:, 9:10], cols[:, 8:9], float(T), None, ALU.mult).then_inc(s_prep.sem, 1)
            dve.wait_ge(s_prep.sem, next(order))
            dve.tensor_scalar(base[:], a[:, 1, :], cols[:, 9:10], None, ALU.add)
            dve.tensor_scalar(pay[:, :, 0], col[:], cols[:, 9:10], None, ALU.add).then_inc(s_prep.sem, 1)
            dve.wait_ge(s_prep.sem, next(order))
            dve.wait_ge(s_row.sem, 1)
            dve.tensor_copy(first_row[:], TPS[0][:, 0:P]).then_inc(s_prep.sem, 1)
            dve.wait_ge(s_prep.sem, next(order))
            dve.tensor_scalar(eq_ff[:], first_row[:], first, None, ALU.is_equal)
            dve.tensor_scalar(eq_lf[:], first_row[:], last_, None, ALU.is_equal).then_inc(s_prep.sem, 1)
            dve.wait_ge(s_prep.sem, next(order))
            dve.tensor_tensor(masked[:], eq_ff[:], part[:], ALU.mult)
            dve.tensor_tensor(masked2[:], eq_lf[:], part[:], ALU.mult).then_inc(s_prep.sem, 1)
            dve.wait_ge(s_prep.sem, next(order))
            dve.tensor_scalar(eq_lf[:], eq_lf[:], cols[:, 2:3], None, ALU.mult).then_inc(s_cntin.sem, 1)
            dve.tensor_reduce(cols[:, 5:6], masked[:], AX.X, ALU.max)
            dve.tensor_reduce(cols[:, 6:7], masked2[:], AX.X, ALU.max).then_inc(s_prep.sem, 1)
            dve.wait_ge(s_prep.sem, next(order))
            for cc, mask in ((5, in_first), (6, in_last)):
                dve.tensor_scalar(cols[:, cc + 5:cc + 6], cols[:, cc:cc + 1], float(FIX), None, ALU.add)
                dve.tensor_scalar(scan[:, 2, :], base[:], -1.0, None, ALU.mult).then_inc(s_prep.sem, 1)
                dve.wait_ge(s_prep.sem, next(order))
                dve.tensor_scalar(scan[:, 3, :], scan[:, 2, :], cols[:, cc + 5:cc + 6], None, ALU.add
                    ).then_inc(s_prep.sem, 1)
                dve.wait_ge(s_prep.sem, next(order))
                dve.tensor_tensor(scan[:, 2, :], scan[:, 3, :], mask[:], ALU.mult).then_inc(s_prep.sem, 1)
                dve.wait_ge(s_prep.sem, next(order))
                dve.tensor_tensor(base[:], base[:], scan[:, 2, :], ALU.add).then_inc(s_prep.sem, 1)
                dve.wait_ge(s_prep.sem, next(order))
            dve.tensor_copy(idx[:, :, 3], base[:])
            dve.tensor_copy(idx[:, :, 0], si[:])
            dve.tensor_scalar(idx[:, :, 1], own, float(N - 1), None, ALU.min)
            dve.tensor_scalar(idx_fix[:, 0:1], first, float(N - 1), None, ALU.min)
            dve.tensor_scalar(cols[:, 12:13], first, -float(SKIP), None, ALU.add)
            dve.tensor_tensor(cols[:, 13:14], cols[:, 9:10], ends_cnt[:, 0:1], ALU.add)
            dve.tensor_scalar(pay_fix[:, 0:1], cols[:, 8:9], float(FIX), None, ALU.add)
            dve.tensor_scalar(tmpa[:], own, -float(SKIP), None, ALU.add).then_inc(s_prep.sem, 1)
            dve.wait_ge(s_prep.sem, next(order))
            dve.tensor_tensor(cols[:, 14:15], cols[:, 12:13], cols[:, 4:5], ALU.mult)
            dve.tensor_scalar(idx_fix[:, 2:3], cols[:, 13:14], -1.0, None, ALU.add)
            dve.tensor_tensor(scan[:, 0, :], tmpa[:], rep[:], ALU.mult).then_inc(s_prep.sem, 1)
            dve.wait_ge(s_prep.sem, next(order))
            dve.tensor_scalar(idx[:, :, 4], scan[:, 0, :], float(SKIP), None, ALU.add)
            dve.tensor_scalar(idx_fix[:, 1:2], cols[:, 14:15], float(SKIP), None, ALU.add)
            dve.wait_ge(s_cnt.sem, 1)
            dve.tensor_copy(pay_fix[:, 1:2], QS[1][:, 0:1]).then_inc(s_idx.sem, 1)

            def degrees():
                dve.wait_ge(s_seen.sem, EU)
                dve.tensor_copy(idx[:, :, 2], seen[:, :, 0])
                dve.tensor_scalar(degs[:, 0:T], seen[:, :, 1], 1.0, None, ALU.add)
                dve.tensor_scalar(degs[:, T:2 * T], pay[:, :, 1], 1.0, None, ALU.add)
                dve.wait_ge(s_idx.sem, 1)
                dve.tensor_scalar(degs[:, 2 * T:], pay_fix[:, 1:2], 1.0, None, ALU.add).then_inc(s_deg.sem, 1)

            def factors():
                dve.wait_ge(s_deg.sem, 1)
                steps = count(1)
                dve.tensor_scalar(dis_t[:].bitcast(I32), degs[:].bitcast(I32), 1, None,
                                  ALU.logical_shift_right).then_inc(s_dis.sem, 1)
                dve.wait_ge(s_dis.sem, next(steps))
                dve.tensor_scalar(dis[:].bitcast(I32), dis_t[:].bitcast(I32), -1, 0x5f3759df, ALU.mult,
                                  ALU.add).then_inc(s_dis.sem, 1)
                dve.wait_ge(s_dis.sem, next(steps))
                for _ in range(3):
                    dve.tensor_tensor(dis_t[:], dis[:], dis[:], ALU.mult).then_inc(s_dis.sem, 1)
                    dve.wait_ge(s_dis.sem, next(steps))
                    dve.scalar_tensor_tensor(out=dis_t[:], in0=dis_t[:], scalar=-0.5, in1=degs[:],
                                             op0=ALU.mult, op1=ALU.mult).then_inc(s_dis.sem, 1)
                    dve.wait_ge(s_dis.sem, next(steps))
                    dve.scalar_tensor_tensor(out=dis[:], in0=dis_t[:], scalar=1.5, in1=dis[:],
                                             op0=ALU.add, op1=ALU.mult).then_inc(s_dis.sem, 1)
                    dve.wait_ge(s_dis.sem, next(steps))
                dve.tensor_copy(fac[:, :, 0], dis[:, 0:T])
                dve.tensor_copy(fac[:, :, 1], dis[:, T:2 * T])
                dve.tensor_tensor(fac[:, :, 2], dis[:, T:2 * T], degs[:, T:2 * T], ALU.mult)
                dve.tensor_copy(fac[:, :, 3], same[:])
                dve.reciprocal(fac[:, :, 4], pay[:, :, 1])
                dve.memset(fac_fix[:, 0:1], 0.0)
                dve.memset(fac_fix[:, 3:4], 0.0)
                dve.tensor_copy(fac_fix[:, 1:2], dis[:, 2 * T:])
                dve.tensor_tensor(fac_fix[:, 2:3], dis[:, 2 * T:], degs[:, 2 * T:], ALU.mult)
                dve.reciprocal(fac_fix[:, 4:5], pay_fix[:, 1:2]).then_inc(s_fac.sem, 1)
                dve.wait_ge(s_fac.sem, 1)

            def stats(c, b, sets, u):
                w = u.c % 2
                bn, tmp = c.bn[b], c.tmp
                per, o3_ = (3, 0) if c is e2 else (6, 3 * b)
                for o, tiles, m in sets:
                    for g in range(m):
                        i = dve.bn_stats(bn[:, o + g, :], tiles[:, g, :])
                i.then_inc(c.s_stats.sem, 1)
                dve.wait_ge(c.s_stats.sem, u.times(per, o3_ + 1))
                dve.tensor_tensor(tmp[:, 0, :], bn[:, :, 1], bn[:, :, 4], ALU.subtract)
                dve.tensor_tensor(tmp[:, 1, :], bn[:, :, 1], bn[:, :, 4], ALU.add)
                dve.scalar_tensor_tensor(out=tmp[:, 2, :], in0=bn[:, :, 2], scalar=D * EPS, in1=bn[:, :, 5],
                                         op0=ALU.add, op1=ALU.add).then_inc(c.s_stats.sem, 1)
                dve.wait_ge(c.s_stats.sem, u.times(per, o3_ + 2))
                dve.scalar_tensor_tensor(out=tmp[:, 0, :], in0=tmp[:, 0, :], scalar=0.25, in1=tmp[:, 0, :],
                                         op0=ALU.mult, op1=ALU.mult)
                dve.tensor_scalar(c.mean[b][:, w, :], tmp[:, 1, :], 0.5, None, ALU.mult).then_inc(c.s_stats.sem, 1)
                dve.wait_ge(c.s_stats.sem, u.times(per, o3_ + 3))
                dve.scalar_tensor_tensor(out=c.var[b][:, w, :], in0=tmp[:, 2, :], scalar=1.0 / D,
                                         in1=tmp[:, 0, :], op0=ALU.mult, op1=ALU.add).then_inc(c.s_var[b].sem, 1)

            def apply_x(c, t, n, w):
                for g in range(G):
                    dve.tensor_scalar(c.u[:, w, g, 0:D], c.x[:, t.slot, g, :], c.mean[0][:, w, g:g + 1], 0.0,
                                      ALU.subtract, ALU.max)
                dve.tensor_tensor(c.u[:, w, :, D], c.var[0][:, w, 0:G], c.rstd[0][:, w, 0:G],
                                  ALU.mult).then_inc(c.s_u.sem, 1)

            def neg_mean(c, u, w):
                dve.scalar_tensor_tensor(out=c.nb[:, w, :], in0=c.mean[0][:, w, G:2 * G], scalar=-1.0,
                                         in1=c.rstd[0][:, w, G:2 * G], op0=ALU.mult,
                                         op1=ALU.mult).then_inc(c.s_nb.sem, 1)

            def apply_x1(c, u, b, o, w, m=G):
                dve.tensor_tensor(c.xb[:, 0:m], c.x[:, u.slot, 0:m], be1b[:, :].unsqueeze(1).broadcast_to([P, m, D]),
                                  ALU.add)
                for g in range(m):
                    i = dve.scalar_tensor_tensor(out=c.z[:, g, :], in0=c.a2[:, u.c % 2, g, :],
                                                 scalar=c.mean[b][:, w, o + g:o + g + 1], in1=g1b[:, :],
                                                 op0=ALU.subtract, op1=ALU.mult)
                i.then_inc(c.s_z.sem, 1)
                dve.wait_ge(c.s_z.sem, c.s_z.upto(u))
                for g in range(m):
                    i = dve.scalar_tensor_tensor(out=c.x1[:, u.slot, g, :], in0=c.z[:, g, :],
                                                 scalar=c.rstd[b][:, w, o + g:o + g + 1], in1=c.xb[:, g, :],
                                                 op0=ALU.mult, op1=ALU.add)
                i.then_inc(c.s_x1.sem, 1)

            def add_out(c, u, m=G):
                dve.wait_ge(c.s_h.sem, c.s_h.upto(u))
                if (u - R).exists:
                    dve.wait_ge(c.o_stored[(u - R).slot], c.o_stored.upto(u - R))
                dve.tensor_tensor(c.o[:, u.slot, 0:m], c.x1[:, u.slot, 0:m], c.h[:, u.slot, 0:m],
                                  ALU.add).then_inc(c.s_o.sem, 1)

            def running_sum(sums_, fct_, msg_, u, counted):
                for g in range(G):
                    before = sums_[:, u.slot, g - 1, :] if g else sums_[:, (u.c - 1) % R, G - 1, :]
                    if u.number == 0 and g == 0:
                        dve.tensor_copy(sums_[:, 0, 0, :], msg_[:, 0, :]).then_inc(counted.sem, 1)
                    else:
                        dve.scalar_tensor_tensor(out=sums_[:, u.slot, g, :], in0=before,
                                                 scalar=fct_[:, u.c % 2, g, 3:4], in1=msg_[:, g, :],
                                                 op0=ALU.mult, op1=ALU.add).then_inc(counted.sem, 1)
                    dve.wait_ge(counted.sem, counted.at(u.times(G, g + 1)))

            def factors_of(fct_, u, counted):
                if u.number == EU:
                    i = dve.tensor_copy(fct_[:, u.c % 2, 0, :], fac_fix[:, :])
                else:
                    i = dve.tensor_copy(fct_[:, u.c % 2], fac[:, bass.ds(u.times(G), G), :])
                i.then_inc(counted.sem, 1)
                dve.wait_ge(counted.sem, counted.upto(u))

            def normalised(to, a_, mean, rstd_, m, o, zi, u, counted_z, counted):
                for g in range(m):
                    i = dve.scalar_tensor_tensor(out=zt[:, zi, g, :], in0=a_[:, g, 0:D],
                                                 scalar=mean[:, o + g:o + g + 1], in1=g0b[:, :],
                                                 op0=ALU.subtract, op1=ALU.mult)
                i.then_inc(counted_z.sem, 1)
                dve.wait_ge(counted_z.sem, counted_z.upto(u))
                for g in range(m):
                    i = dve.scalar_tensor_tensor(out=to[:, g, :], in0=zt[:, zi, g, :],
                                                 scalar=rstd_[:, o + g:o + g + 1], in1=be0b[:, :],
                                                 op0=ALU.mult, op1=ALU.add)
                i.then_inc(counted.sem, 1)

            def chain_stats(c, t, n):
                w, v = t.c % 2, (t.c - 1) % 2
                e1 = c is edge
                on = t.within(n + 3)
                if not on:
                    return
                fix = 1 if t.number == n else G
                sets = []
                if t.within(n):
                    dve.wait_ge(c.loaded[t.slot], c.loaded.upto(t, 16 * G if e1 else 16))
                    sets.append((0, c.x[:, t.slot], G))
                if e1 and t.within(n + 1):
                    dve.wait_ge(xd_loaded[t.slot], xd_loaded.upto(t, 16 * G, 16 * fix))
                    sets.append((2 * G, xd[:, t.slot], fix))
                if (t - 3).within(n):
                    dve.wait_ge(c.s_x1.sem, c.s_x1.upto(t - 3))
                    sets.append((G, c.x1[:, (t - 3).slot], G))
                stats(c, 0, sets, t)
                b_on = t.within(n + 2)
                sets = []
                if (t - 1).within(n):
                    dve.wait_ge(c.s_a1.sem, c.s_a1.upto(t - 1))
                    sets.append((0, c.a1[:, v, :, 0:D], G))
                if e1 and (t - 1).within(n + 1):
                    dve.wait_ge(s_ad.sem, s_ad.upto(t - 1))
                    sets.append((2 * G, ad[:, v], 1 if (t - 1).number == n else G))
                if (t - 2).within(n):
                    dve.wait_ge(c.s_a2.sem, c.s_a2.upto(t - 2))
                    sets.append((G, c.a2[:, w], G))
                if b_on:
                    if sets:
                        stats(c, 1, sets, t)
                    else:
                        stats(c, 1, [(0, g1b[:, :].unsqueeze(1), 1)], t)

            def chain_apply(c, t, n):
                w, v = t.c % 2, (t.c - 1) % 2
                e1 = c is edge
                on, b_on = t.within(n + 3), t.within(n + 2)
                if not on:
                    if (t - 4).within(n) and not e1:
                        add_out(c, t - 4)
                    return
                fix = 1 if t.number == n else G
                dve.wait_ge(c.s_rstd[0].sem, c.s_rstd[0].upto(t))
                if t.within(n):
                    apply_x(c, t, n, w)
                if (t - 3).within(n):
                    neg_mean(c, t - 3, w)
                if e1 and t.within(n + 1):
                    sums_of_unit(t, n, w, fix)
                if (t - 4).within(n) and not e1:
                    add_out(c, t - 4)
                if not b_on:
                    return
                dve.wait_ge(c.s_rstd[1].sem, c.s_rstd[1].upto(t))
                if (t - 1).within(n):
                    dve.tensor_tensor(c.a1[:, v, :, D], c.var[1][:, w, 0:G], c.rstd[1][:, w, 0:G],
                                      ALU.mult).then_inc(c.s_a1_std.sem, 1)
                if (t - 2).within(n):
                    apply_x1(c, t - 2, 1, G, w)
                if e1:
                    u = t - 1
                    if u.within(n):
                        if (u - R).exists:
                            dve.wait_ge(zs_stored[(u - R).slot], zs_stored.upto(u - R))
                        normalised(zs[:, u.slot], c.a1[:, v], c.mean[1][:, w], c.rstd[1][:, w], G, 0, 0, u,
                                   s_zt, s_zs)
                    if u.within(n + 1):
                        if (u - R).exists:
                            dve.wait_ge(zd_stored[(u - R).slot], zd_stored.upto(u - R))
                        normalised(zd[:, u.slot], ad[:, v], c.mean[1][:, w], c.rstd[1][:, w],
                                   1 if u.number == n else G, 2 * G, 1, u, s_ztd, s_zd)

            def sums_of_unit(t, n, w, m):
                c = edge
                factors_of(fct, t, s_fct)
                if m == G:
                    dve.tensor_tensor(coef[:, w, 0, :], c.rstd[0][:, w, 0:G], fct[:, w, :, 0], ALU.mult)
                dve.tensor_tensor(coef[:, w, 1, 0:m], c.rstd[0][:, w, 2 * G:2 * G + m], fct[:, w, 0:m, 1],
                                  ALU.mult)
                for g in range(m):
                    i = dve.tensor_scalar(ud[:, g, :], xd[:, t.slot, g, :],
                                          c.mean[0][:, w, 2 * G + g:2 * G + g + 1], 0.0, ALU.subtract, ALU.max)
                i.then_inc(s_ud.sem, 1)
                dve.wait_ge(s_ud.sem, s_ud.upto(t))
                if m == G:
                    dve.wait_ge(c.s_u.sem, c.s_u.upto(t))
                    for g in range(G):
                        i = dve.tensor_scalar(msg[:, g, :], c.u[:, w, g, 0:D], coef[:, w, 0, g:g + 1], None,
                                              ALU.mult)
                    i.then_inc(s_msg.sem, 1)
                    dve.wait_ge(s_msg.sem, s_msg.upto(t))
                    if (t - R).exists:
                        dve.wait_ge(sum_stored[(t - R).slot], sum_stored.upto(t - R))
                    running_sum(sums, fct, msg, t, s_sum)
                else:
                    dve.wait_ge(s_tot.sem, 1)
                for g in range(m):
                    total = sums[:, t.slot, g, :] if m == G else QS[3][:, 4 * D:5 * D]
                    dve.scalar_tensor_tensor(out=bd[:, w, g, 0:D], in0=ud[:, g, :],
                                             scalar=coef[:, w, 1, g:g + 1], in1=total, op0=ALU.mult,
                                             op1=ALU.add)
                dve.tensor_copy(bd[:, w, 0:m, D], fct[:, w, 0:m, 2]).then_inc(s_bd.sem, 1)

            def stats2(t):
                c = e2
                if t.number == 0:
                    dve.wait_ge(edge.s_h.sem, edge.s_h.upto(At(None, EU - 1)))
                if t.within(EU + 3, 1):
                    k = t - 1
                    sets = []
                    if k.within(EU + 1):
                        dve.wait_ge(c.s_a2.sem, c.s_a2.upto(k))
                        sets.append((0, c.a2[:, k.c % 2], 1 if k.number == EU else G))
                    if (t - 2).within(EU + 1):
                        dve.wait_ge(c.s_x1.sem, c.s_x1.upto(t - 2))
                        sets.append((G, c.x1[:, (t - 2).slot], 1 if (t - 2).number == EU else G))
                    stats(c, 0, sets, k)

            def chain2(t):
                c, w = e2, t.c % 2
                if t.within(EU + 1):
                    m = 1 if t.number == EU else G
                    factors_of(fct2, t, s_fct2)
                    dve.wait_ge(zd2_loaded[t.slot], zd2_loaded.upto(t))
                    if m == G:
                        dve.wait_ge(zs2_laid[t.slot], zs2_laid.upto(t, 16 * G))
                        for g in range(G):
                            i = dve.tensor_scalar(msg[:, g, :], zs2[:, t.slot, g, :], fct2[:, w, g, 0:1], None,
                                                  ALU.mult)
                        i.then_inc(s_msg2.sem, 1)
                        dve.wait_ge(s_msg2.sem, s_msg2.upto(t))
                        if (t - R).exists:
                            dve.wait_ge(sum2_stored[(t - R).slot], sum2_stored.upto(t - R))
                        running_sum(sums2, fct2, msg, t, s_sum2)
                    else:
                        dve.wait_ge(s_tot.sem, 2)
                    for g in range(m):
                        total = sums2[:, t.slot, g, :] if m == G else QS[3][:, 4 * D:5 * D]
                        dve.scalar_tensor_tensor(out=c.u[:, w, g, 0:D], in0=zd2[:, t.slot, g, :],
                                                 scalar=fct2[:, w, g, 1:2], in1=total, op0=ALU.mult,
                                                 op1=ALU.add)
                    dve.tensor_copy(c.u[:, w, 0:m, D], fct2[:, w, 0:m, 2]).then_inc(c.s_u.sem, 1)
                if (t - 3).within(EU + 1):
                    add_out(c, t - 3, 1 if (t - 3).number == EU else G)
                if t.within(EU + 3, 1):
                    k = t - 1
                    dve.wait_ge(c.s_rstd[0].sem, c.s_rstd[0].upto(k))
                    if k.within(EU + 1):
                        dve.wait_ge(c.loaded[k.slot], c.loaded.upto(k))
                        apply_x1(c, k, 0, 0, k.c % 2, 1 if k.number == EU else G)
                    if (t - 2).within(EU + 1):
                        neg_mean(c, t - 2, k.c % 2)

            def step(s):
                a, b = s - S1, s - S2
                chain_stats(node, s, NU)
                chain_stats(edge, a, EU)
                stats2(b)
                chain_apply(node, s, NU)
                chain_apply(edge, a, EU)
                chain2(b)
                if s.number == S1 - 2:
                    degrees()
                if s.number == S1 - 1:
                    factors()

            run_steps(dve, step)

            def copy_attr(u):
                dve.wait_ge(s_tp3.sem, s_tp3.upto(u))
                if (u - 1).exists:
                    dve.wait_ge(s_q3.sem, s_q3.upto(u - 1))
                dve.tensor_copy(ut[0:DE, 2, :], TPS[2][0:DE, :]).then_inc(s_ut3.sem, 1)

            def step3(u):
                if not u.within(EU + 1):
                    return
                fix = u.number == EU
                factors_of(fct3, u, s_fct3)
                if u.number == 0:
                    copy_attr(u)
                if (u + 1).within(EU):
                    copy_attr(u + 1)
                if not fix:
                    q = QALL[:, 1024 * (u.c % 2):1024 * (u.c % 2) + 1024].rearrange(
                        "p (b f) -> p b f", b=2)[:, :, 0:4 * D].rearrange("p b (g f) -> p b g f", g=2)
                    dve.wait_ge(s_exp3.sem, s_exp3.upto(u))
                    dve.tensor_scalar(eg3[:], eg3[:], 1.0, None, ALU.add).then_inc(s_e13.sem, 1)
                    dve.wait_ge(s_e13.sem, s_e13.upto(u))
                    dve.reciprocal(gt3[:], eg3[:]).then_inc(s_rc3.sem, 1)
                    dve.wait_ge(s_ln3.sem, s_ln3.upto(u))
                    for b in range(2):
                        i = dve.scalar_tensor_tensor(out=ab3[:, 2 * b:2 * b + 2, :], in0=q[:, b, :, D:2 * D],
                                                     scalar=0.0, in1=ln3[:, 2 * b:2 * b + 2, :],
                                                     op0=ALU.max, op1=ALU.add)
                    i.then_inc(s_m3.sem, 1)
                    dve.wait_ge(s_m3.sem, s_m3.upto(u))
                    dve.wait_ge(s_rc3.sem, s_rc3.upto(u))
                    dve.tensor_tensor(msg[:], ab3[:], gt3[:], ALU.mult).then_inc(s_gt3.sem, 1)
                    dve.wait_ge(s_gt3.sem, s_gt3.upto(u))
                    if (u - R).exists:
                        dve.wait_ge(sum3_stored[(u - R).slot], sum3_stored.upto(u - R))
                    running_sum(sums3, fct3, msg, u, s_sum3)
                    dve.wait_ge(rest3_loaded[u.slot], rest3_loaded.upto(u, 32))
                else:
                    dve.wait_ge(s_tot.sem, 3)
                    dve.wait_ge(rest3_loaded[u.slot], rest3_loaded.upto(u, 32, 16))
                m = 1 if fix else G
                if (u - R).exists:
                    dve.wait_ge(out_put[(u - R).slot], out_put.upto(u - R, 16 * G))
                for g in range(m):
                    total = QS[3][:, 4 * D:5 * D] if fix else sums3[:, u.slot, g, :]
                    i = dve.scalar_tensor_tensor(out=res3[:, u.slot, g, :], in0=total,
                                                 scalar=fct3[:, u.c % 2, g, 4:5], in1=o3[:, u.slot, g, :],
                                                 op0=ALU.mult, op1=ALU.add)
                i.then_inc(s_res3.sem, 1)

            run_steps(dve, step3, SEGMENTS3)


_INS = ["x", "src", "dst", "edge_attr_64", "L0_gnn_W0", "L0_gnn_b0", "L0_gnn_g0", "L0_gnn_be0",
        "L0_gnn_W1", "L0_gnn_b1", "L0_gnn_g1", "L0_gnn_be1", "L1_gnn_W_e", "L1_gnn_b_e",
        "L1_gnn_W_n", "L1_gnn_b_n"]


def kernel(**inputs):
    import numpy as _np
    import concourse.bacc as _bacc
    from concourse import mybir as _mybir
    from concourse.bass_utils import run_bass_kernel_spmd as _run

    nc = _bacc.Bacc("TRN2", target_bir_lowering=False, num_devices=1)
    arrays, args = {}, []
    for name in _INS:
        a = _np.ascontiguousarray(inputs[name])
        arrays[f"in_{name}_dram"] = a
        args.append(nc.dram_tensor(f"in_{name}_dram", a.shape, _mybir.dt.from_np(a.dtype),
                                   kind="ExternalInput").ap())
    args.append(nc.dram_tensor("out_0_dram", (N, D), F32, kind="ExternalOutput").ap())
    build(nc, *args)
    r = _run(nc, [arrays], core_ids=[0])
    return r.results[0]["out_0_dram"]
```

```python
from contextlib import ExitStack
from itertools import count

import numpy as np
import concourse.bass as bass
from concourse import mybir

F32 = mybir.dt.float32
I32 = mybir.dt.int32
ALU = mybir.AluOpType
ACT = mybir.ActivationFunctionType
AX = mybir.AxisListType

P = 128
N, D = 100000, 96
E, DE = 25000, 64
G = 4
R = 4
DA = D + 1
DZ = D + 2
T = -(-E // P)
ES = P * T
FIX = ES
ROWS = ES + P
EU = T // G
NU = -(-N // (P * G))
FILL = 125
LAST = N - P * G
SKIP = 1 << 20
EPS = 1e-5

PUT, TAKE = 0, 52
S1 = 108
S2 = S1 + EU + 3
END = S2 + EU + 6
END3 = EU + 4
RANKED = 3 + P * (5 * (T // 7) + 2)
assert T % 7 == 0 and T % G == 0 and EU % R == 1 and not any(s % R for s in (PUT, TAKE, S1, S2))
SEGMENTS = [("steps", 0, 8), ("loop", 8, 48), ("steps", 48, 60), ("loop", 60, 100),
            ("steps", 100, S1 + 8), ("loop", S1 + 8, S1 + 48), ("steps", S1 + 48, S2 + 8),
            ("loop", S2 + 8, NU - 4), ("steps", NU - 4, END)]
SEGMENTS3 = [("steps", 0, 8), ("loop", 8, 44), ("steps", 44, END3)]


class At:

    def __init__(self, j, c, span=(0, 1)):
        self.j, self.c, self.span = j, c, span

    def __add__(self, k):
        return At(self.j, self.c + k, self.span)

    def __sub__(self, k):
        return self + -k

    @property
    def slot(self):
        return self.c % R

    def times(self, a, b=0):
        return a * self.c + b if self.j is None else self.j * (R * a) + (a * self.c + b)

    def laps(self, a, b=0):
        return a * (self.c // R) + b if self.j is None else self.j * a + (a * (self.c // R) + b)

    def within(self, n, first=0):
        lo, hi = (R * k + self.c for k in (self.span[0], self.span[1] - 1))
        yes = [first <= v < n for v in (lo, hi)]
        assert yes[0] == yes[1] and not (lo < first and hi >= n)
        return yes[0]

    @property
    def exists(self):
        return self.j is not None or self.c >= 0

    @property
    def number(self):
        return self.c if self.j is None else None


class Count:

    def __init__(self, sem, base=0):
        self.sem, self.base = sem, base

    def at(self, value):
        return value + self.base

    def upto(self, u, per=1):
        return u.times(per, per + self.base)

    def again(self, total):
        return Count(self.sem, self.base + total)


class Slots:

    def __init__(self, sems, base=(0,) * R):
        self.sems, self.base = sems, base

    def __getitem__(self, k):
        return self.sems[k]

    def upto(self, u, each=16, last=None):
        return u.laps(each, (each if last is None else last) + self.base[u.slot])

    def all(self, k, units, each=16):
        return each * len(range(k, units, R)) + self.base[k]

    def again(self, *uses):
        base = [b + sum(each * len([u for u in range(lo, hi) if u % R == k]) for lo, hi, each in uses)
                for k, b in enumerate(self.base)]
        return Slots(self.sems, base)


def run_steps(eng, step, segments=SEGMENTS):
    for kind, lo, hi in segments:
        if kind == "steps":
            for s in range(lo, hi):
                step(At(None, s))
        else:
            assert lo % R == 0 and hi % R == 0
            with eng.Fori(lo // R, hi // R) as j:
                for c in range(R):
                    step(At(j, c, (lo // R, hi // R)))


def build(nc, x, src, dst, edge_attr, W0, b0, g0, be0, W1, b1, g1, be1, W_e, b_e, W_n, b_n, out):
    with ExitStack() as ctx:
        def sb(name, shape, dt=F32):
            return ctx.enter_context(nc.sbuf_tensor(name, shape, dt))

        def sem(name):
            return Count(ctx.enter_context(nc.semaphore(name)))

        def ring_sems(name):
            return Slots([ctx.enter_context(nc.semaphore(f"{name}{k}")) for k in range(R)])

        def dram(name, shape, dt=F32):
            return nc.dram_tensor(name, shape, dt).ap()

        dst_sorted = dram("dst_sorted", [1, ES + 2], I32)
        src_sorted = dram("src_sorted", [1, ES], I32)
        attr_sorted = dram("attr_sorted", [ES, DE])
        attr_given = dram("attr_given", [ES, DE])
        node_tab = dram("node_tab", [N, 2])
        sum_tab = [dram(f"sum_tab{k}", [ES, DA if k == 1 else D]) for k in range(3)]
        z_src = dram("z_src", [ES, DZ])
        h_src = dram("h_src", [ES, D])
        x_dst = dram("x_dst", [ROWS, D])
        z_dst = dram("z_dst", [ROWS, DZ])
        h_dst = dram("h_dst", [ROWS, D])
        o_dst = dram("o_dst", [ROWS, D])

        def edge_units(table, width=D):
            return table[0:ES].rearrange("(p t) d -> p (t d)", p=P)

        ident = sb("ident", [P, P])
        idle = sb("idle", [P, 2, 8, R])
        w0 = sb("w0", [DA, D])
        w1n = sb("w1n", [DA, D])
        w1 = sb("w1", [D, D])
        w1e = sb("w1e", [DZ, D])
        wa = sb("wa", [DA, 2 * D])
        wb = sb("wb", [D, 2 * D])
        wc = sb("wc", [DE, 2 * D])
        g0b, be0b, g1b, be1b = (sb(n, [P, D]) for n in ("g0b", "be0b", "g1b", "be1b"))
        g0c = sb("g0c", [D, 1])
        centre = sb("centre", [D, DA])
        pick = sb("pick", [D, DA])
        w1g = sb("w1g", [DA, D])
        mhalf = sb("mhalf", [P, 3 * G])
        zeros = sb("zeros", [P, 2 * D])
        pads = sb("pads", [1, 3, ES - E + 2], I32)
        fill = sb("fill", [P, N // FILL])

        di = sb("di", [P, 3, T], I32)
        si = sb("si", [P, T], I32)
        df = sb("df", [P, 3, T])
        same = sb("same", [P, T])
        rep = sb("rep", [P, T])
        in_first = sb("in_first", [P, T])
        in_last = sb("in_last", [P, T])
        col = sb("col", [P, T])
        base = sb("base", [P, T])
        tmpa = sb("tmpa", [P, T])
        iota_i = sb("iota_i", [P, T], I32)
        part_i = sb("part_i", [P, P], I32)
        part = sb("part", [P, P])
        cols = sb("cols", [P, 16])
        first_row = sb("first_row", [P, P])
        eq_ff = sb("eq_ff", [P, P])
        eq_lf = sb("eq_lf", [P, P])
        ends_cnt = sb("ends_cnt", [P, 2])
        idx = sb("idx", [P, T, 5], I32)
        idx_fix = sb("idx_fix", [P, 4], I32)
        pay = sb("pay", [P, T, 2])
        pay_fix = sb("pay_fix", [P, 2])
        seen = sb("seen", [P, T, 2])
        fac = sb("fac", [P, T, 5])
        fac_fix = sb("fac_fix", [P, 5])
        degs = sb("degs", [P, 2 * T + 1])
        dis = sb("dis", [P, 2 * T + 1])
        dis_t = sb("dis_t", [P, 2 * T + 1])

        falls = sb("falls", [1, 1], I32)
        sevens = sb("sevens", [P, 8])
        rank_i = sb("rank_i", [P, 2, T], I32)

        def ring(name, width=D, slots=R, dt=F32, g=G):
            return sb(name, [P, slots, g, width], dt)

        class Chain:

            def __init__(self, name, sets):
                self.late = 1 if name == "node" else 0
                self.x = ring(name + "_x") if name != "e2" else edge.x
                self.u = ring(name + "_u", DA if name != "e2" else DZ, 2)
                self.a1 = ring(name + "_a1", DZ, 2) if name != "e2" else None
                self.a2 = ring(name + "_a2", D, 4 if name == "node" else 2)
                self.x1 = ring(name + "_x1") if name != "e2" else edge.x1
                self.h = ring(name + "_h", D, 4)
                self.o = ring(name + "_o") if name != "edge" else None
                self.bn = [sb(f"{name}_bn{k}", [P, sets, 6]) for k in "ab"]
                self.nmean = [sb(f"{name}_nmean{k}", [P, 2, sets]) for k in "ab"]
                self.var = [sb(f"{name}_var{k}", [P, 2, sets]) for k in "ab"]
                self.rstd = [sb(f"{name}_rstd{k}", [P, 2, sets]) for k in "ab"]
                self.tmp = sb(name + "_tmp", [P, 3, sets])
                self.nb = sb(name + "_nb", [P, 2, G])
                self.z = sb(name + "_z", [P, G, D])
                self.xb = sb(name + "_xb", [P, G, D])
                self.loaded = (ring_sems(name + "_loaded") if name != "e2"
                               else xd_stored.again((0, EU + 1, 16)))
                if name != "edge":
                    self.o_stored = ring_sems(name + "_o_stored")
                self.s_stats = sem(name + "_stats")
                self.s_var = [sem(name + "_var_a")]
                self.s_rstd = [sem(name + "_rstd_a")]
                self.s_u, self.s_x1, self.s_nb = (sem(f"{name}_{k}") for k in ("u", "x1", "nb"))
                self.s_h = sem(name + "_h") if name != "e2" else s_rowin.again(1)
                self.s_z = sem(name + "_z") if name != "e2" else s_cntin.again(1)
                self.s_tp1, self.s_ut1, self.s_q1 = (sem(f"{name}_{k}") for k in ("tp1", "ut1", "q1"))
                self.s_a2 = sem(name + "_a2")
                if name != "e2":
                    self.s_var.append(sem(name + "_var_b"))
                    self.s_rstd.append(sem(name + "_rstd_b"))
                    self.s_a1_std, self.s_a1 = sem(name + "_a1_std"), sem(name + "_a1")
                    self.s_tp2, self.s_ut2, self.s_q2 = (sem(f"{name}_{k}") for k in ("tp2", "ut2", "q2"))
                    self.s_relu = sem(name + "_relu")
                if name != "edge":
                    self.s_xb = sem("node_xb") if name == "node" else s_falls.again(1)
                if name != "edge":
                    self.s_o = sem(name + "_o") if name != "e2" else s_w1in.again(1)

        node = Chain("node", 2 * G)
        edge = Chain("edge", 3 * G)
        s_w1in, s_rowin, s_cntin, s_const, s_falls = (
            sem(n) for n in ("w1_in", "row_in", "cnt_in", "const", "falls"))
        xd_stored = ring_sems("xd_st")
        e2 = Chain("e2", 2 * G)

        xd = ring("xd")
        ud = sb("ud", [P, G, D])
        bd = ring("bd", DA, 2)
        ad = ring("ad", DZ, 2)
        msg = sb("msg", [P, G, D])
        sums = ring("sums")
        coef = sb("coef", [P, 2, 2, G])
        fct = sb("fct", [P, 2, G, 5])
        ends = sb("ends", [P, 3, DA])
        ixr = sb("ixr", [P, R, G, 5], I32)
        ixr3 = sb("ixr3", [P, R, G, 5], I32)
        payr = sb("payr", [P, R, G, 2])
        seenr = sb("seenr", [P, R, G, 2])
        zs2 = ring("zs2", DZ)
        zd2 = ring("zd2", DZ)
        coef2 = sb("coef2", [P, 2, 2, G])
        msg2 = sb("msg2", [P, G, DA])
        sums2 = ring("sums2", DA)
        fct2 = sb("fct2", [P, 2, G, 5])
        hs3 = ring("hs3", DA)
        o3, res3 = ring("o3"), ring("res3")
        at3 = edge.h[:, :, :, 0:DE]
        fct3 = sb("fct3", [P, 2, G, 5])
        hd3, sums3 = xd, sums
        eg3, ab3, ex3, ln3, gt3 = node.z, node.xb, edge.z, edge.xb, e2.z
        firsts, masked, masked2 = (msg[:, :, :].rearrange("p g d -> p (g d)")[:, k * P:(k + 1) * P]
                                   for k in range(3))
        own_t = [b[:, :, :, :].rearrange("p s g d -> p (s g d)")[:, 0:7 * T].rearrange(
            "p (k t) -> p k t", k=7) for b in (sums, sums2, o3)]
        others_f, others_no, own_no, rank_f = (
            res3[:, :, :, :].rearrange("p s g d -> p (s g d)")[:, k * T:(k + 1) * T] for k in range(4))
        others_i = iota_i[:, :]
        scan, scanb = (b[:, :, :, :].rearrange("p s g d -> p (s g d)")[:, 0:4 * T].rearrange(
            "p (k t) -> p k t", k=4) for b in (zs2, zd2))

        ut = sb("ut", [DZ, 4, P * G])
        TPS = [ctx.enter_context(nc.psum_tensor(f"tp{k}", [P, P * G], F32)) for k in range(4)]
        QALL = ctx.enter_context(nc.psum_tensor("q", [P, 4 * 512], F32))
        QS = [QALL[:, 512 * k:512 * k + 512] for k in range(4)]

        def qv(k, g=None):
            v = QS[k][:, 0:G * D].rearrange("p (g d) -> p g d", g=G)
            return v if g is None else v[:, g, :]

        s_staged, s_w, s_wz, s_ident = (
            sem(n) for n in ("staged", "weights", "wz", "ident_ready"))
        s_prep = sem("prep")
        s_falls_sum, s_order = sem("falls_sum"), sem("order_known")
        s_others, s_others_used, s_rank = sem("others_in"), sem("others_used"), sem("rank")
        s_attr, s_rows_in, s_resorted, s_reloaded = (
            sem(n) for n in ("attr_staged", "attr_rows_in", "resorted", "reloaded"))
        s_sort_copied = sem("sort_copied")
        s_wmm, s_w1n = sem("wmm"), sem("w1n_ready")
        s_edges = sem("edges_loaded")
        s_row, s_cnt = sem("row_ready"), sem("cnt_ready")
        s_idx, s_tab0, s_fac = sem("idx_ready"), sem("tab_zeroed"), sem("fac_ready")
        s_copied, s_put, s_got = sem("ix_copied"), ring_sems("tab_put"), ring_sems("tab_got")
        s_putfix = sem("tab_put_fix")
        s_seen = sem("seen_ready")
        s_deg, s_dis = sem("deg_ready"), sem("dis_ready")
        s_zero = sem("zeroed")
        xd_loaded = ring_sems("xd_loaded")
        sum_stored, zs_stored, zd_stored, hs_stored = (
            ring_sems(n) for n in ("sum_st", "zs_st", "zd_st", "hs_st"))
        s_ix1, s_fct, s_msg, s_sum, s_ud, s_bd, s_ad, s_zd, s_udt, s_utd, s_qd = (
            sem(n) for n in ("ix1", "fct", "msg", "sum", "ud", "bd_ready", "ad_ready",
                             "zd_ready", "tpd", "utd", "qd"))
        s_ends, s_tot, s_coef, s_coef2 = (sem(n) for n in ("ends_in", "tot", "coef", "coef2"))
        sum2_stored, hd_stored = ring_sems("sum2_st"), ring_sems("hd_st")
        s_ix2, s_fct2, s_msg2, s_sum2 = (c.again(1) for c in (s_wmm, s_row, s_cnt, s_w1n))
        zs2_laid = s_put.again((0, EU, 16 * G))
        zs2_loaded = zs_stored.again((0, EU, 16))
        zd2_loaded = zd_stored.again((0, EU + 1, 16))
        hs3_laid = zs2_laid.again((0, EU, 16 * G))
        hd3_got = s_got.again((0, EU, 16 * G))
        out_put = xd_loaded.again((0, EU, 16 * G), (EU, EU + 1, 16))
        hs3_loaded = hs_stored.again((0, EU, 16))
        rest3_loaded = hd_stored.again((0, EU + 1, 16))
        sum3_stored = sum_stored.again((0, EU, 16))
        s_ix3, s_ixput3 = s_ix1.again(EU), s_copied.again(3 * EU)
        s_tp3, s_ut3, s_q3 = (c.again(EU) for c in (edge.s_tp1, edge.s_ut1, edge.s_q1))
        s_exp3, s_abs3, s_ea3, s_ln3 = (c.again(EU) for c in (edge.s_a1, edge.s_ut2, edge.s_a2, edge.s_h))
        s_m3, s_rc3, s_gt3, s_e13 = (c.again(k) for c, k in (
            (s_msg, EU), (edge.s_u, EU), (edge.s_x1, EU), (s_ud, EU + 1)))
        s_sum3, s_fct3, s_res3 = s_sum.again(G * EU), s_fct.again(EU + 1), s_bd.again(EU + 1)
        s_outfix = s_putfix.again(16)

        block = ctx.enter_context(nc.Block())

        def node_rows(t, u):
            if u.j is None and u.c == NU - 1:
                return t[LAST:N, :].rearrange("(p g) d -> p g d", g=G)
            full = t[0:(NU - 1) * P * G, :].rearrange("(u p g) d -> u p g d", p=P, g=G)
            return full[u.times(1)]

        def edge_rows(t, u, width=D):
            if u.j is None and u.c == EU:
                return t[FIX:FIX + P, :].rearrange("(p g) d -> p g d", g=1)
            v = t[0:ES, :].rearrange("(p t) d -> p t d", p=P)
            return v[:, bass.ds(u.times(G), G), :]

        @block.sync
        def _(sp):
            for t, v in ((w0[0:D, :], W0), (w0[D:DA, :], b0.rearrange("(a d) -> a d", a=1)),
                         (w1[:, :], W1), (w1e[DA:DZ, :], b1.rearrange("(a d) -> a d", a=1)),
                         (w1g[D:DA, :], b1.rearrange("(a d) -> a d", a=1)),
                         (wa[0:D, 0:D], W_e[0:D, :]), (wa[0:D, D:2 * D], W_n[0:D, :]),
                         (wa[D:DA, 0:D], b_e.rearrange("(a d) -> a d", a=1)),
                         (wa[D:DA, D:2 * D], b_n.rearrange("(a d) -> a d", a=1)),
                         (wb[:, 0:D], W_e[D:2 * D, :]), (wb[:, D:2 * D], W_n[D:2 * D, :]),
                         (wc[:, 0:D], W_e[2 * D:, :]), (wc[:, D:2 * D], W_n[2 * D:, :]),
                         (g0c[:, :], g0.rearrange("(d a) -> d a", a=1)),
                         (g0b[:, :], g0.partition_broadcast(P)), (be0b[:, :], be0.partition_broadcast(P)),
                         (g1b[:, :], g1.partition_broadcast(P)), (be1b[:, :], be1.partition_broadcast(P))):
                sp.dma_start(t, v).then_inc(s_w.sem, 16)
            sp.wait_ge(s_const.sem, 1)
            sp.dma_start(pick[:, D:DA], be0.rearrange("(d a) -> d a", a=1)).then_inc(s_wz.sem, 16)
            sp.wait_ge(s_zero.sem, 1)
            sp.dma_start(dst_sorted[:, 1:1 + E], dst.rearrange("(a e) -> a e", a=1)).then_inc(s_staged.sem, 16)
            sp.dma_start(src_sorted[:, 0:E], src.rearrange("(a e) -> a e", a=1)).then_inc(s_staged.sem, 16)
            sp.dma_start(dst_sorted[:, 0:1], pads[:, 0, 0:1]).then_inc(s_staged.sem, 16)
            sp.dma_start(dst_sorted[:, ES + 1:ES + 2], pads[:, 0, 1:2]).then_inc(s_staged.sem, 16)
            sp.dma_start(dst_sorted[:, 1 + E:1 + ES], pads[:, 1, 0:ES - E]).then_inc(s_staged.sem, 16)
            sp.dma_start(src_sorted[:, E:ES], pads[:, 2, 0:ES - E]).then_inc(s_staged.sem, 16)
            sp.wait_ge(s_staged.sem, 16 * 6)
            for k in range(3):
                o = (1, 0, 2)[k]
                sp.dma_start(di[:, k, :], dst_sorted[0, o:o + ES].rearrange("(p t) -> p t", p=P)
                             ).then_inc(s_edges.sem, 16)
            sp.dma_start(si[:, :], src_sorted[0, :].rearrange("(p t) -> p t", p=P)).then_inc(s_edges.sem, 16)

            for k in range(2):
                sp.dma_start(node_tab[k * (N // 2):(k + 1) * (N // 2), :].rearrange(
                    "(p r) c -> p (r c)", p=FILL), fill[0:FILL, :]).then_inc(s_tab0.sem, 16)
            sp.dma_start(attr_sorted[0:E, :], edge_attr).then_inc(s_attr.sem, 16)
            sp.dma_start(attr_sorted[E:ES, :], zeros[0:ES - E, 0:DE]).then_inc(s_attr.sem, 16)

            sp.wait_ge(s_order.sem, 1)
            unsorted = sp.value_load(falls[0:1, 0:1])
            with sp.If(unsorted > 0):
                sp.wait_ge(s_attr.sem, 16 * 2)
                sp.dma_start(attr_given, attr_sorted).then_inc(s_attr.sem, 16)
                of_partition = dst_sorted[0, 1:1 + ES].rearrange("(p t) -> p t", p=P)
                sp.dma_start(others_i, of_partition[0].partition_broadcast(P)).then_inc(s_others.sem, 16)
                with sp.Fori(1, P) as c:
                    sp.wait_ge(s_others_used.sem, c * 1)
                    sp.dma_start(others_i, of_partition[c].partition_broadcast(P)).then_inc(s_others.sem, 16)
                sp.wait_ge(s_attr.sem, 16 * 3)
                given = attr_given[:, :].rearrange("(p t) d -> p t d", p=P)
                sp.dma_start(edge.h[:, 0, :, 0:DE], given[:, 0:G, :]).then_inc(s_rows_in.sem, 16)
                with sp.Fori(1, EU) as j:
                    sp.wait_ge(s_resorted.sem, j * (16 * 3 * G))
                    sp.dma_start(edge.h[:, 0, :, 0:DE], given[:, bass.ds(j * G, G), :]
                                 ).then_inc(s_rows_in.sem, 16)
                sp.wait_ge(s_resorted.sem, EU * 16 * 3 * G)
                for k in range(3):
                    o = (1, 0, 2)[k]
                    sp.dma_start(di[:, k, :], dst_sorted[0, o:o + ES].rearrange("(p t) -> p t", p=P)
                                 ).then_inc(s_reloaded.sem, 16)
                sp.dma_start(si[:, :], src_sorted[0, :].rearrange("(p t) -> p t", p=P)
                             ).then_inc(s_reloaded.sem, 16)

            def load_node(u):
                if u.within(NU):
                    if (u - R).exists:
                        sp.wait_ge(node.s_xb.sem, node.s_xb.upto(u - R))
                    sp.dma_start(node.x[:, u.slot], node_rows(x, u)).then_inc(node.loaded[u.slot], 16)

            def store_node(u):
                if u.within(NU):
                    sp.wait_ge(node.s_o.sem, node.s_o.upto(u))
                    if u.j is None and u.c == NU - 1:
                        for slot in range(R):
                            sp.wait_ge(node.o_stored[slot], node.o_stored.all(slot, NU - 1))
                    sp.dma_start(node_rows(out, u), node.o[:, u.slot]).then_inc(node.o_stored[u.slot], 16)

            def store(table, tile, sems, u, last, ready, per=1):
                if u.within(last):
                    sp.wait_ge(ready.sem, ready.upto(u, per))
                    fix = u.j is None and u.c == EU
                    slot = u.c % tile.shape[1]
                    sp.dma_start(edge_rows(table, u), tile[:, slot, 0:1 if fix else G, :]
                                 ).then_inc(sems[u.slot], 16)

            def load2(u):
                if u.within(EU + 1):
                    fix = u.j is None and u.c == EU
                    n = 1 if fix else G
                    if u.j is None and u.c == 0:
                        for slot in range(R):
                            sp.wait_ge(zs_stored[slot], zs_stored.all(slot, EU))
                        for slot in range(R):
                            sp.wait_ge(xd_stored[slot], xd_stored.all(slot, EU + 1))
                        for slot in range(R):
                            sp.wait_ge(zd_stored[slot], zd_stored.all(slot, EU + 1))
                    if (u - R).exists:
                        sp.wait_ge(e2.s_u.sem, e2.s_u.upto(u - R))
                    if not fix:
                        sp.dma_start(zs2[:, u.slot], edge_rows(z_src, u)).then_inc(zs2_loaded[u.slot], 16)
                    sp.dma_start(zd2[:, u.slot, 0:n, :], edge_rows(z_dst, u)).then_inc(zd2_loaded[u.slot], 16)
                    if (u - 4).exists:
                        sp.wait_ge(e2.s_x1.sem, e2.s_x1.upto(u - 4))
                    sp.dma_start(e2.x[:, u.slot, 0:n, :], edge_rows(x_dst, u)).then_inc(e2.loaded[u.slot], 16)

            load_node(At(None, 0))

            def step(s):
                load_node(s + 1)
                a, b = s - S1, s - S2
                store_node(s - 6)
                store(sum_tab[0], sums, sum_stored, a, EU, s_sum, G)
                store(x_dst, xd, xd_stored, a, EU + 1, s_bd)
                store(z_src, edge.a1, zs_stored, a - 1, EU, edge.s_a1_std)
                store(z_dst, ad, zd_stored, a - 1, EU + 1, s_zd)
                load2(b + 1)
                store(h_src, edge.h, hs_stored, a - 4, EU, edge.s_h)
                store(sum_tab[1], sums2, sum2_stored, b, EU, s_sum2, G)
                store(h_dst, e2.h, hd_stored, b - 3, EU + 1, e2.s_h)
                store(o_dst, e2.o, e2.o_stored, b - 4, EU + 1, e2.s_o)

            run_steps(sp, step)

            for slot in range(R):
                sp.wait_ge(hs_stored[slot], hs_stored.all(slot, EU))
            for slot in range(R):
                sp.wait_ge(hd_stored[slot], hd_stored.all(slot, EU + 1))
            for slot in range(R):
                sp.wait_ge(e2.o_stored[slot], e2.o_stored.all(slot, EU + 1))

            def load3(u):
                if u.within(EU + 1):
                    fix = u.j is None and u.c == EU
                    if (u - 4).exists:
                        sp.wait_ge(s_res3.sem, s_res3.upto(u - 4))
                    if not fix:
                        sp.dma_start(hs3[:, u.slot, :, 0:D], edge_rows(h_src, u)).then_inc(hs3_loaded[u.slot], 16)
                        sp.dma_start(at3[:, u.slot], edge_rows(attr_sorted, u)).then_inc(rest3_loaded[u.slot], 16)
                    sp.dma_start(o3[:, u.slot, 0:1 if fix else G, :], edge_rows(o_dst, u)
                                 ).then_inc(rest3_loaded[u.slot], 16)

            sp.wait_ge(s_attr.sem, 16 * 2)
            load3(At(None, 0))
            load3(At(None, 1))
            load3(At(None, 2))

            def step3(s):
                load3(s + 3)
                store(sum_tab[2], sums3, sum3_stored, s, EU, s_sum3, G)

            run_steps(sp, step3, SEGMENTS3)
            for slot in range(R):
                sp.wait_ge(node.o_stored[slot], node.o_stored.all(slot, NU))

        @block.gpsimd
        def _(pool):
            pool.memset(ident[:], 0.0).then_inc(s_ident.sem, 1)
            pool.wait_ge(s_ident.sem, 1)
            pool.affine_select(out=ident[:], in_=ident[:], compare_op=ALU.not_equal, fill=1.0, base=0,
                               pattern=[[-1, P]], channel_multiplier=1).then_inc(s_ident.sem, 1)
            pool.iota(iota_i[:], pattern=[[1, T]], base=0, channel_multiplier=0).then_inc(s_ident.sem, 1)
            pool.iota(part_i[:], pattern=[[1, P]], base=0, channel_multiplier=0).then_inc(s_ident.sem, 1)
            pool.iota(idx_fix[:, 3:4], pattern=[[0, 1]], base=0, channel_multiplier=1).then_inc(s_ident.sem, 1)

            def rstd(c, b, u, sets):
                w = u.c % 2
                pool.wait_ge(c.s_var[b].sem, c.s_var[b].upto(u))
                pool.tensor_tensor(c.rstd[b][:, w, 0:sets], c.var[b][:, w, 0:sets], mhalf[:, 0:sets],
                                   ALU.pow).then_inc(c.s_rstd[b].sem, 1)

            def gather(to, table, index, bound, landed_):
                pool.indirect_dma_start(out=to, out_offset=None, in_=table,
                                        in_offset=bass.IndirectOffsetOnAxis(ap=index, axis=0),
                                        bounds_check=bound, oob_is_err=False).then_inc(landed_, 16)

            def scatter(table, index, rows, bound, landed_):
                pool.indirect_dma_start(out=table, out_offset=bass.IndirectOffsetOnAxis(ap=index, axis=0),
                                        in_=rows, in_offset=None,
                                        bounds_check=bound, oob_is_err=False).then_inc(landed_, 16)

            pool.memset(idle[:], 0.0).then_inc(s_ident.sem, 1)
            pool.wait_ge(s_ident.sem, 6)

            def before_dmas(k, u):
                if u.number is None:
                    pool.tensor_tensor(idle[:, 1, k, u.slot:u.slot + 1], idle[:, 0, k, u.slot:u.slot + 1],
                                       idle[:, 0, k, u.slot:u.slot + 1], ALU.add)

            pool.wait_ge(s_order.sem, 1)
            unsorted = pool.value_load(falls[0:1, 0:1])
            with pool.If(unsorted > 0):
                pool.wait_ge(s_rank.sem, RANKED)
                with pool.Fori(0, EU) as j:
                    pool.wait_ge(s_rows_in.sem, j * 16 + 16)
                    now = bass.ds(j * G, G)
                    pool.tensor_copy(ixr[:, 0, :, 0], rank_i[:, 0, now]).then_inc(s_sort_copied.sem, 1)
                    pool.tensor_copy(ixr[:, 0, :, 1], rank_i[:, 1, now]).then_inc(s_sort_copied.sem, 1)
                    pool.tensor_copy(ixr[:, 0, :, 2], di[:, 0, now]).then_inc(s_sort_copied.sem, 1)
                    pool.tensor_copy(ixr[:, 0, :, 3], si[:, now]).then_inc(s_sort_copied.sem, 1)
                    pool.wait_ge(s_sort_copied.sem, j * 4 + 4)
                    pool.tensor_tensor(idle[:, 1, 5, 0:1], idle[:, 0, 5, 0:1], idle[:, 0, 5, 0:1], ALU.add)
                    for g in range(G):
                        scatter(dst_sorted.rearrange("a (e b) -> (a e) b", b=1), ixr[:, 0, g, 1:2], ixr[:, 0, g, 2:3],
                                ES, s_resorted.sem)
                        scatter(src_sorted.rearrange("a (e b) -> (a e) b", b=1), ixr[:, 0, g, 0:1], ixr[:, 0, g, 3:4],
                                ES - 1, s_resorted.sem)
                        scatter(attr_sorted, ixr[:, 0, g, 0:1], edge.h[:, 0, g, 0:DE], ES - 1, s_resorted.sem)
                    pool.wait_ge(s_resorted.sem, j * (16 * 3 * G) + 16 * 3 * G)
                    pool.tensor_tensor(idle[:, 1, 5, 1:2], idle[:, 0, 5, 1:2], idle[:, 0, 5, 1:2], ALU.add)

            def put_tab(u):
                if not u.within(EU):
                    return
                if (u - R).exists:
                    pool.wait_ge(s_put[(u - R).slot], s_put.upto(u - R, 16 * G))
                pool.tensor_copy(ixr[:, u.slot, :, 4], idx[:, bass.ds(u.times(G), G), 4]).then_inc(s_copied.sem, 1)
                pool.tensor_copy(payr[:, u.slot], pay[:, bass.ds(u.times(G), G), :]).then_inc(s_copied.sem, 1)
                pool.wait_ge(s_copied.sem, s_copied.upto(u, 2))
                before_dmas(0, u)
                for g in range(G):
                    scatter(node_tab, ixr[:, u.slot, g, 4:5], payr[:, u.slot, g, :], N - 1, s_put[u.slot])

            def take_tab(u):
                if u.within(EU + R, R):
                    v = u - R
                    pool.wait_ge(s_got[v.slot], s_got.upto(v, 16 * G))
                    pool.tensor_copy(seen[:, bass.ds(v.times(G), G), :], seenr[:, v.slot]).then_inc(s_seen.sem, 1)
                if not u.within(EU):
                    return
                pool.tensor_copy(ixr[:, u.slot, :, 0], idx[:, bass.ds(u.times(G), G), 0]).then_inc(s_copied.sem, 1)
                pool.wait_ge(s_copied.sem, u.times(1, 2 * EU + 1))
                if u.number is None or u.number >= R:
                    pool.wait_ge(s_seen.sem, u.times(1, 1 - R))
                before_dmas(1, u)
                for g in range(G):
                    gather(seenr[:, u.slot, g, :], node_tab, ixr[:, u.slot, g, 0:1], N - 1, s_got[u.slot])

            def gather_sources(u):
                if not u.within(EU):
                    return
                if (u - R).exists:
                    pool.wait_ge(edge.loaded[(u - R).slot], edge.loaded.upto(u - R, 16 * G))
                if (u - R).exists:
                    pool.wait_ge(xd_loaded[(u - R).slot], xd_loaded.upto(u - R, 16 * G))
                pool.tensor_copy(ixr[:, u.slot], idx[:, bass.ds(u.times(G), G), :]).then_inc(s_ix1.sem, 1)
                pool.wait_ge(s_ix1.sem, s_ix1.upto(u))
                if (u - R).exists:
                    pool.wait_ge(edge.s_x1.sem, edge.s_x1.upto(u - R))
                before_dmas(2, u)
                for g in range(G):
                    gather(edge.x[:, u.slot, g, :], x, ixr[:, u.slot, g, 0:1], N - 1, edge.loaded[u.slot])

            def gather_dests(u):
                if not u.within(EU + 1):
                    return
                if (u - R).exists:
                    pool.wait_ge(xd_stored[(u - R).slot], xd_stored.upto(u - R))
                if (u - R).exists:
                    pool.wait_ge(s_bd.sem, s_bd.upto(u - R))
                if u.number == EU:
                    gather(xd[:, u.slot, 0, :], x, idx_fix[:, 0:1], N - 1, xd_loaded[u.slot])
                    return
                before_dmas(3, u)
                for g in range(G):
                    gather(xd[:, u.slot, g, :], x, ixr[:, u.slot, g, 1:2], N - 1, xd_loaded[u.slot])

            def gather_ends(k, stored):
                for slot in range(R):
                    pool.wait_ge(stored[slot], stored.all(slot, EU))
                gather(ends[:, k, 0:sum_tab[k].shape[1]], sum_tab[k], idx_fix[:, 2:3], ES - 1, s_ends.sem)

            def add_be1(u):
                if not u.within(EU + 1):
                    return
                m = 1 if u.number == EU else G
                pool.wait_ge(e2.loaded[u.slot], e2.loaded.upto(u))
                if (u - 1).exists:
                    pool.wait_ge(e2.s_x1.sem, e2.s_x1.upto(u - 1))
                pool.tensor_tensor(e2.xb[:, 0:m], e2.x[:, u.slot, 0:m],
                                   be1b[:, :].unsqueeze(1).broadcast_to([P, m, D]),
                                   ALU.add).then_inc(e2.s_xb.sem, 1)

            def add_out(u):
                if not u.within(EU + 1):
                    return
                m = 1 if u.number == EU else G
                pool.wait_ge(e2.s_h.sem, e2.s_h.upto(u))
                if (u - R).exists:
                    pool.wait_ge(e2.o_stored[(u - R).slot], e2.o_stored.upto(u - R))
                pool.tensor_tensor(e2.o[:, u.slot, 0:m], e2.x1[:, u.slot, 0:m], e2.h[:, u.slot, 0:m],
                                   ALU.add).then_inc(e2.s_o.sem, 1)

            def lay2(u):
                if not u.within(EU):
                    return
                if (u - R).exists:
                    pool.wait_ge(zs2_laid[(u - R).slot], zs2_laid.upto(u - R, 16 * G))
                pool.tensor_copy(ixr3[:, u.slot], idx[:, bass.ds(u.times(G), G), :]).then_inc(s_ix2.sem, 1)
                pool.wait_ge(s_ix2.sem, s_ix2.upto(u))
                pool.wait_ge(zs2_loaded[u.slot], zs2_loaded.upto(u))
                before_dmas(4, u)
                for g in range(G):
                    gather(zs2[:, u.slot, g, :], z_dst, ixr3[:, u.slot, g, 2:3], ROWS - 1, zs2_laid[u.slot])

            def step(s):
                a, b = s - S1, s - S2
                if s.number == PUT:
                    pool.wait_ge(s_idx.sem, 1)
                    pool.wait_ge(s_tab0.sem, 32)
                    scatter(node_tab, idx_fix[:, 1:2], pay_fix[:, :], N - 1, s_putfix.sem)
                if s.number == TAKE:
                    for slot in range(R):
                        pool.wait_ge(s_put[slot], s_put.all(slot, EU, 16 * G))
                    pool.wait_ge(s_putfix.sem, 16)
                if a.number == EU:
                    gather_ends(0, sum_stored)
                if b.number == EU:
                    gather_ends(1, sum2_stored)
                if s.number == S2 - 1:
                    for slot in range(R):
                        pool.wait_ge(zd_stored[slot], zd_stored.all(slot, EU + 1))
                if s.within(NU + 4):
                    rstd(node, 0, s, 2 * G)
                if s.within(NU + 3):
                    rstd(node, 1, s, 2 * G)
                if a.within(EU + 3):
                    rstd(edge, 0, a, 3 * G)
                if a.within(EU + 2):
                    rstd(edge, 1, a, 3 * G)
                if b.within(EU + 3, 1):
                    rstd(e2, 0, b - 1, 2 * G)
                add_be1(b - 1)
                add_out(b - 3)
                put_tab(s - PUT)
                take_tab(s - TAKE)
                if s.number == S1 - 1:
                    pool.wait_ge(s_fac.sem, 1)
                gather_sources(a + 1)
                gather_dests(a + 1)
                lay2(b + 1)

            run_steps(pool, step)

            def gather3(u):
                if not u.within(EU):
                    return
                if (u - R).exists:
                    pool.wait_ge(hs3_laid[(u - R).slot], hs3_laid.upto(u - R, 16 * G))
                if (u - R).exists:
                    pool.wait_ge(hd3_got[(u - R).slot], hd3_got.upto(u - R, 16 * G))
                pool.tensor_copy(ixr[:, u.slot], idx[:, bass.ds(u.times(G), G), :]).then_inc(s_ix3.sem, 1)
                pool.wait_ge(s_ix3.sem, s_ix3.upto(u))
                if (u - R).exists:
                    pool.wait_ge(s_tp3.sem, s_tp3.upto(u - R))
                before_dmas(6, u)
                for g in range(G):
                    gather(hd3[:, u.slot, g, :], h_dst, ixr[:, u.slot, g, 3:4], ROWS - 1, hd3_got[u.slot])
                pool.wait_ge(hs3_loaded[u.slot], hs3_loaded.upto(u))
                before_dmas(5, u)
                for g in range(G):
                    gather(hs3[:, u.slot, g, 0:D], h_dst, ixr[:, u.slot, g, 2:3], ROWS - 1, hs3_laid[u.slot])

            def put3(u):
                if u.number == EU:
                    pool.wait_ge(s_res3.sem, s_res3.upto(u))
                    scatter(out, idx_fix[:, 1:2], res3[:, u.slot, 0, :], N - 1, s_outfix.sem)
                if not u.within(EU):
                    return
                if (u - R).exists:
                    pool.wait_ge(out_put[(u - R).slot], out_put.upto(u - R, 16 * G))
                pool.tensor_copy(ixr3[:, u.slot, :, 4], idx[:, bass.ds(u.times(G), G), 4]).then_inc(s_ixput3.sem, 1)
                pool.wait_ge(s_ixput3.sem, s_ixput3.upto(u))
                pool.wait_ge(s_res3.sem, s_res3.upto(u))
                before_dmas(7, u)
                for g in range(G):
                    scatter(out, ixr3[:, u.slot, g, 4:5], res3[:, u.slot, g, :], N - 1, out_put[u.slot])

            for slot in range(R):
                pool.wait_ge(hd_stored[slot], hd_stored.all(slot, EU + 1))
            gather3(At(None, 0))

            def step3(s):
                if s.number == 0:
                    for slot in range(R):
                        pool.wait_ge(node.o_stored[slot], node.o_stored.all(slot, NU))
                gather3(s + 1)
                put3(s - 2)
                if s.number == EU:
                    gather_ends(2, sum3_stored)

            run_steps(pool, step3, SEGMENTS3)
            for slot in range(R):
                pool.wait_ge(out_put[slot], out_put.all(slot, EU, 16 * G))
            pool.wait_ge(s_outfix.sem, s_outfix.at(16))

        @block.scalar
        def _(act):
            def copy_ut(k, n, before, ready, u):
                act.wait_ge(before.sem, before.upto(u))
                nc.scalar.copy(ut[0:n, k, :], TPS[k][0:n, :]).then_inc(ready.sem, 1)

            def tanh(to, k, scale, before, ready, u, n=G):
                act.wait_ge(before.sem, before.upto(u))
                for g in range(n):
                    i = nc.scalar.activation(to[:, g, :], qv(k, g), ACT.Tanh, scale=scale[:, g:g + 1])
                i.then_inc(ready.sem, 1)

            def relu_x1(c, k, first, u, t):
                act.wait_ge(c.s_nb.sem, c.s_nb.upto(u))
                for g in range(G):
                    i = nc.scalar.activation(c.h[:, u.slot, g, :], c.x1[:, u.slot, g, :], ACT.Relu,
                                             bias=c.nb[:, t.c % 2, g:g + 1],
                                             scale=c.rstd[k][:, t.c % 2, first + g:first + g + 1])
                i.then_inc(c.s_h.sem, 1)

            def relu_x(c, t, n):
                w = t.c % 2
                if t.within(n):
                    act.wait_ge(c.s_var[0].sem, c.s_var[0].upto(t))
                    for g in range(G):
                        i = nc.scalar.activation(c.u[:, w, g, 0:D], c.x[:, t.slot, g, :], ACT.Relu,
                                                 bias=c.nmean[0][:, w, g:g + 1])
                    i.then_inc(c.s_relu.sem, 1)
                if c is edge and t.within(n + 1):
                    act.wait_ge(c.s_var[0].sem, c.s_var[0].upto(t))
                    for g in range(1 if t.number == n else G):
                        i = nc.scalar.activation(ud[:, g, :], xd[:, t.slot, g, :], ACT.Relu,
                                                 bias=c.nmean[0][:, w, 2 * G + g:2 * G + g + 1])
                    i.then_inc(s_ud.sem, 1)

            def chain(c, k, t, n):
                w = t.c % 2
                if t.within(n):
                    copy_ut(k, DA, c.s_tp1, c.s_ut1, t)
                if (t - 1).within(n):
                    copy_ut(k + 1, DA, c.s_tp2, c.s_ut2, t - 1)
                if c is edge and t.within(n + 1):
                    copy_ut(k, DA, s_udt, s_utd, t)
                if c is node and (t - 4).within(n):
                    if (t - 4 - R).exists:
                        act.wait_ge(c.s_o.sem, c.s_o.upto(t - 4 - R))
                    relu_x1(c, 0, G, t - 4, t)
                if t.within(n):
                    if c is edge and (t - 2).exists:
                        act.wait_ge(zs_stored[(t - 2).slot], zs_stored.upto(t - 2))
                    tanh(c.a1[:, w, :, 0:D], k, c.rstd[0][:, w, 0:G], c.s_q1, c.s_a1, t)
                if (t - 1).within(n):
                    ring_ = c.a2.shape[1]
                    if (t - 1 - ring_).exists:
                        act.wait_ge(c.s_x1.sem, c.s_x1.upto(t - 1 - ring_))
                    tanh(c.a2[:, (t.c - 1) % ring_], k + 1, c.rstd[1][:, w, 0:G], c.s_q2, c.s_a2, t - 1)
                if c is edge and t.within(n + 1):
                    m = 1 if t.number == n else G
                    if (t - 2).exists:
                        act.wait_ge(zd_stored[(t - 2).slot], zd_stored.upto(t - 2))
                    tanh(ad[:, w, :, 0:D], k, fct[:, w, :, 1], s_qd, s_ad, t, m)
                if c is edge and (t - 3).within(n):
                    if (t - 3 - R).exists:
                        act.wait_ge(hs_stored[(t - 3 - R).slot], hs_stored.upto(t - 3 - R))
                    relu_x1(c, 0, G, t - 3, t)

            def chain2(t):
                if t.within(EU + 1):
                    w, m = t.c % 2, 1 if t.number == EU else G
                    copy_ut(2, DZ, e2.s_tp1, e2.s_ut1, t)
                    if (t - 2).exists:
                        act.wait_ge(e2.s_x1.sem, e2.s_x1.upto(t - 2))
                    tanh(e2.a2[:, w], 2, fct2[:, w, :, 1], e2.s_q1, e2.s_a2, t, m)
                if (t - 2).within(EU + 1):
                    if (t - 2 - R).exists:
                        act.wait_ge(hd_stored[(t - 2 - R).slot], hd_stored.upto(t - 2 - R))
                    if (t - 2 - R).exists:
                        act.wait_ge(e2.s_o.sem, e2.s_o.upto(t - 2 - R))
                    relu_x1(e2, 0, G, t - 2, t - 1)

            def step(s):
                relu_x(node, s, NU)
                relu_x(edge, s - S1, EU)
                chain(node, 0, s, NU)
                chain(edge, 2, s - S1, EU)
                chain2(s - S2)

            run_steps(act, step)

            def copy_rows(u):
                act.wait_ge(s_tp3.sem, s_tp3.upto(u))
                if (u - 1).exists:
                    act.wait_ge(s_q3.sem, s_q3.upto(u - 1))
                nc.scalar.copy(ut[0:DA, 0, :], TPS[0][0:DA, :]).then_inc(s_ut3.sem, 1)
                nc.scalar.copy(ut[0:D, 1, :], TPS[1][0:D, :]).then_inc(s_ut3.sem, 1)

            def step3(u):
                if not u.within(EU):
                    return
                if u.number == 0:
                    copy_rows(u)
                act.wait_ge(s_q3.sem, s_q3.upto(u))
                q = QALL[:, 1024 * (u.c % 2):1024 * (u.c % 2) + 1024].rearrange(
                    "p (b f) -> p b f", b=2)[:, :, 0:4 * D].rearrange("p b (g f) -> p b g f", g=2)
                if (u - 1).exists:
                    act.wait_ge(s_gt3.sem, s_gt3.upto(u - 1))
                for b in range(2):
                    i = nc.scalar.activation(eg3[:, 2 * b:2 * b + 2, :], q[:, b, :, 0:D], ACT.Exp, scale=-1.0)
                i.then_inc(s_exp3.sem, 1)
                for b in range(2):
                    i = nc.scalar.activation(ab3[:, 2 * b:2 * b + 2, :], q[:, b, :, D:2 * D], ACT.Abs)
                i.then_inc(s_abs3.sem, 1)
                act.wait_ge(s_abs3.sem, s_abs3.upto(u))
                nc.scalar.activation(ex3[:], ab3[:], ACT.Exp, scale=-1.0).then_inc(s_ea3.sem, 1)
                if (u + 1).within(EU):
                    copy_rows(u + 1)
                act.wait_ge(s_ea3.sem, s_ea3.upto(u))
                nc.scalar.activation(ln3[:], ex3[:], ACT.Ln, bias=1.0).then_inc(s_ln3.sem, 1)

            run_steps(act, step3, SEGMENTS3)

        @block.tensor
        def _(pe):
            def turn(rows, k, n, ready, m=G):
                for g in range(m):
                    i = pe.transpose(TPS[k][0:n, g * P:(g + 1) * P], rows[:, g, :], ident[:, :])
                i.then_inc(ready.sem, 1)

            def product(k, w, ready, m=G):
                for g in range(m):
                    i = pe.matmul(qv(k, g), ut[0:w.shape[0], k, g * P:(g + 1) * P], w[:, :], start=True, stop=True)
                i.then_inc(ready.sem, 1)

            def fix_total(k, last):
                pe.wait_ge(s_ends.sem, 16 * (k + 1))
                width = last.shape[1]
                out_ = QS[3][:, 4 * D:4 * D + width]
                pe.matmul(out_, eq_ff[:, :], ends[:, k, 0:width], start=True, stop=False)
                pe.matmul(out_, eq_lf[:, :], last, start=False, stop=True).then_inc(s_tot.sem, 1)

            pe.wait_ge(s_ident.sem, 2)
            pe.wait_ge(s_w1in.sem, 1)
            pe.wait_ge(s_wz.sem, 16)
            pe.matmul(QS[0][0:DA, 0:D], centre[:, :], w1g[0:D, :], start=True, stop=False)
            pe.matmul(QS[0][0:DA, 0:D], pick[:, :], w1[:, :], start=False, stop=True).then_inc(s_wmm.sem, 1)
            pe.wait_ge(s_falls.sem, 1)
            pe.matmul(QS[2][0:1, 0:1], cols[:, 7:8], hs3[:, 0, 0, D:DA], start=True, stop=True
                      ).then_inc(s_falls_sum.sem, 1)
            pe.wait_ge(s_rowin.sem, 1)
            pe.transpose(TPS[0][:, 0:P], firsts[:, :], ident[:, :]).then_inc(s_row.sem, 1)
            pe.wait_ge(s_cntin.sem, 1)
            pe.matmul(QS[1][:, 0:1], eq_ff[:, :], ends_cnt[:, 0:1], start=True, stop=False)
            pe.matmul(QS[1][:, 0:1], eq_lf[:, :], ends_cnt[:, 1:2], start=False, stop=True).then_inc(s_cnt.sem, 1)
            pe.wait_ge(s_w1n.sem, 1)
            pe.wait_ge(s_idx.sem, 1)

            def chain(c, k, t, n):
                w = t.c % 2
                if t.within(n):
                    pe.wait_ge(c.s_relu.sem, c.s_relu.upto(t))
                    pe.wait_ge(c.s_u.sem, c.s_u.upto(t))
                    turn(c.u[:, w], k, DA, c.s_tp1)
                if (t - 1).within(n):
                    pe.wait_ge(c.s_a1_std.sem, c.s_a1_std.upto(t - 1))
                    turn(c.a1[:, (t.c - 1) % 2, :, 0:DA], k + 1, DA, c.s_tp2)
                if t.within(n):
                    pe.wait_ge(c.s_ut1.sem, c.s_ut1.upto(t))
                    if c is edge:
                        if (t - 1).exists:
                            pe.wait_ge(s_ad.sem, s_ad.upto(t - 1))
                    else:
                        if (t - 1).exists:
                            pe.wait_ge(c.s_a1.sem, c.s_a1.upto(t - 1))
                    product(k, w0, c.s_q1)
                if c is edge and t.within(n + 1):
                    m = 1 if t.number == n else G
                    pe.wait_ge(s_bd.sem, s_bd.upto(t))
                    turn(bd[:, w], k, DA, s_udt, m)
                if (t - 1).within(n):
                    pe.wait_ge(c.s_ut2.sem, c.s_ut2.upto(t - 1))
                    if (t - 2).exists:
                        pe.wait_ge(c.s_a2.sem, c.s_a2.upto(t - 2))
                    product(k + 1, w1n, c.s_q2)
                if c is edge and t.within(n + 1):
                    pe.wait_ge(s_utd.sem, s_utd.upto(t))
                    if (t - 1 if t.number == n else t).exists:
                        pe.wait_ge(c.s_a1.sem, c.s_a1.upto(t - 1 if t.number == n else t))
                    product(k, w0, s_qd, m)

            def step(s):
                chain(node, 0, s, NU)
                a, t = s - S1, s - S2
                if a.number == EU:
                    fix_total(0, sums[:, (EU - 1) % R, G - 1, :])
                chain(edge, 2, a, EU)
                if t.number == EU:
                    fix_total(1, sums2[:, (EU - 1) % R, G - 1, :])
                if t.within(EU + 1):
                    m = 1 if t.number == EU else G
                    pe.wait_ge(e2.s_u.sem, e2.s_u.upto(t))
                    turn(e2.u[:, t.c % 2], 2, DZ, e2.s_tp1, m)
                    pe.wait_ge(e2.s_ut1.sem, e2.s_ut1.upto(t))
                    if (t - 1).exists:
                        pe.wait_ge(e2.s_a2.sem, e2.s_a2.upto(t - 1))
                    product(2, w1e, e2.s_q1, m)

            run_steps(pe, step)

            def step3(u):
                if u.number == EU:
                    fix_total(2, sums3[:, (EU - 1) % R, G - 1, :])
                if not u.within(EU):
                    return
                pe.wait_ge(rest3_loaded[u.slot], rest3_loaded.upto(u, 32))
                pe.wait_ge(hd3_got[u.slot], hd3_got.upto(u, 16 * G))
                pe.wait_ge(hs3_laid[u.slot], hs3_laid.upto(u, 16 * G))
                if (u - 1).exists:
                    pe.wait_ge(s_ut3.sem, s_ut3.upto(u - 1, 3))
                for g in range(G):
                    c = slice(g * P, (g + 1) * P)
                    pe.transpose(TPS[0][0:DA, c], hs3[:, u.slot, g, :], ident[:, :])
                    pe.transpose(TPS[1][0:D, c], hd3[:, u.slot, g, :], ident[:, :])
                    i = pe.transpose(TPS[2][0:DE, c], at3[:, u.slot, g, :], ident[:, :])
                i.then_inc(s_tp3.sem, 1)
                pe.wait_ge(s_ut3.sem, s_ut3.upto(u, 3))
                if (u - 2).exists:
                    pe.wait_ge(s_gt3.sem, s_gt3.upto(u - 2))
                for g in range(G):
                    c = slice(g * P, (g + 1) * P)
                    q = 1024 * (u.c % 2) + 512 * (g // 2) + 2 * D * (g % 2)
                    o = QALL[:, q:q + 2 * D]
                    pe.matmul(o, ut[0:DA, 0, c], wa[:, :], start=True, stop=False)
                    pe.matmul(o, ut[0:D, 1, c], wb[:, :], start=False, stop=False)
                    i = pe.matmul(o, ut[0:DE, 2, c], wc[:, :], start=False, stop=True)
                i.then_inc(s_q3.sem, 1)

            run_steps(pe, step3, SEGMENTS3)

        @block.vector
        def _(dve):
            order = count(1)

            for t, v in ((mhalf, -0.5), (zeros, 0.0), (centre[:, 0:D], -1.0 / D), (centre[:, D:DA], 0.0),
                         (pick[:, 0:D], 0.0), (hs3[:, :, :, D], 1.0), (pads[:, 0, 0:1], -1),
                         (pads[:, 0, 1:2], N + 1), (pads[:, 1, :], N), (pads[:, 2, :], 0)):
                dve.memset(t if isinstance(t, bass.AP) else t[:], v)
            f = fill[:, :].rearrange("p (r c) -> p r c", c=2)
            dve.memset(f[:, :, 0], float(SKIP))
            dve.memset(f[:, :, 1], 0.0)
            for c in (node, edge, e2):
                for b in c.bn:
                    dve.memset(b[:], 1.0)
            dve.memset(tmpa[:], 0.0).then_inc(s_prep.sem, 1)
            dve.wait_ge(s_prep.sem, next(order))
            dve.memset(cols[:], 0.0).then_inc(s_zero.sem, 1)
            dve.memset(dis[:, 0:1], 0.0).then_inc(s_const.sem, 1)
            dve.wait_ge(s_w.sem, 16 * 18)
            dve.tensor_scalar(w1g[0:D, :], w1[:, :], g0c[:, 0:1], None, ALU.mult).then_inc(s_w1in.sem, 1)
            dve.wait_ge(s_wmm.sem, 1)
            dve.wait_ge(s_w1in.sem, 1)
            dve.tensor_tensor(w1n[:, :], QS[0][0:DA, 0:D], w1g[:, :], ALU.add)
            dve.tensor_tensor(w1e[0:D, :], QS[0][0:D, 0:D], w1g[0:D, :], ALU.add)
            dve.tensor_copy(w1e[D:DA, :], QS[0][D:DA, 0:D]).then_inc(s_w1n.sem, 1)

            dve.wait_ge(s_edges.sem, 16 * 4)
            dve.wait_ge(s_ident.sem, 5)
            dve.tensor_copy(df[:], di[:])
            dve.tensor_copy(col[:], iota_i[:])
            dve.tensor_copy(cols[:, 8:9], idx_fix[:, 3:4]).then_inc(s_prep.sem, 1)
            dve.wait_ge(s_prep.sem, next(order))
            own, before, after = df[:, 0, :], df[:, 1, :], df[:, 2, :]
            dve.tensor_tensor(tmpa[:], own, after, ALU.is_gt).then_inc(s_prep.sem, 1)
            dve.wait_ge(s_prep.sem, next(order))
            dve.tensor_reduce(cols[:, 7:8], tmpa[:], AX.X, ALU.max).then_inc(s_falls.sem, 1)
            dve.wait_ge(s_falls_sum.sem, 1)
            dve.tensor_copy(falls[:, :], QS[2][0:1, 0:1]).then_inc(s_order.sem, 1)
            dve.wait_ge(s_order.sem, 1)
            unsorted = dve.value_load(falls[0:1, 0:1])
            with dve.If(unsorted > 0):
                dve.memset(rank_f, 0.0)
                dve.tensor_copy(others_no, col[:])
                dve.tensor_scalar(cols[:, 9:10], cols[:, 8:9], float(T), None, ALU.mult).then_inc(s_rank.sem, 1)
                dve.wait_ge(s_rank.sem, 1)
                dve.tensor_scalar(own_no, col[:], cols[:, 9:10], None, ALU.add).then_inc(s_rank.sem, 1)
                dve.wait_ge(s_rank.sem, 2)
                with dve.Fori(0, P) as c:
                    per = 5 * (T // 7) + 2
                    dve.wait_ge(s_others.sem, c * 16 + 16)
                    dve.tensor_copy(others_f, others_i).then_inc(s_rank.sem, 1)
                    dve.wait_ge(s_rank.sem, c * per + 3)
                    dve.memset(sevens[:, 7:8], 0.0)
                    with dve.Fori(0, T // 7) as j:
                        now = bass.ds(j * 7, 7)
                        lower, moved, less = own_t
                        at = c * per + j * 5 + 3

                        def of_all(row):
                            return row.unsqueeze(1).broadcast_to([P, 7, T])

                        def of_own(row):
                            return row[:, now].unsqueeze(2).broadcast_to([P, 7, T])

                        dve.tensor_tensor(lower, of_all(others_no), of_own(own_no), ALU.is_lt
                                          ).then_inc(s_rank.sem, 1)
                        dve.wait_ge(s_rank.sem, at + 1)
                        dve.scalar_tensor_tensor(out=moved, in0=lower, scalar=-0.5, in1=of_all(others_f),
                                                 op0=ALU.mult, op1=ALU.add).then_inc(s_rank.sem, 1)
                        dve.wait_ge(s_rank.sem, at + 2)
                        dve.tensor_tensor(less, moved, of_own(own), ALU.is_lt).then_inc(s_rank.sem, 1)
                        dve.wait_ge(s_rank.sem, at + 3)
                        dve.tensor_reduce(sevens[:, 0:7], less, AX.X, ALU.add).then_inc(s_rank.sem, 1)
                        dve.wait_ge(s_rank.sem, at + 4)
                        dve.tensor_tensor(rank_f[:, now], rank_f[:, now], sevens[:, 0:7], ALU.add
                                          ).then_inc(s_rank.sem, 1)
                        dve.wait_ge(s_rank.sem, at + 5)
                        dve.memset(sevens[:, 7:8], 0.0)
                    dve.tensor_scalar(others_no, others_no, float(T), None, ALU.add).then_inc(s_rank.sem, 1)
                    dve.wait_ge(s_rank.sem, c * per + (2 + per))
                    dve.memset(sevens[:, 7:8], 0.0).then_inc(s_others_used.sem, 1)
                dve.tensor_copy(rank_i[:, 0, :], rank_f)
                dve.tensor_scalar(rank_i[:, 1, :], rank_f, 1.0, None, ALU.add).then_inc(s_rank.sem, 1)
                dve.wait_ge(s_reloaded.sem, 16 * 4)
                dve.tensor_copy(df[:], di[:]).then_inc(s_rank.sem, 1)
                dve.wait_ge(s_rank.sem, RANKED + 1)

            dve.tensor_copy(part[:], part_i[:])
            first, last_ = df[:, 0, 0:1], df[:, 0, T - 1:T]
            dve.tensor_copy(firsts[:], first.broadcast_to([P, P])).then_inc(s_rowin.sem, 1)
            dve.tensor_tensor(same[:], own, before, ALU.is_equal)
            dve.tensor_tensor(tmpa[:], own, after, ALU.is_equal)
            dve.tensor_scalar(in_first[:], own, first, None, ALU.is_equal)
            dve.tensor_scalar(in_last[:], own, last_, None, ALU.is_equal)
            dve.tensor_tensor(cols[:, 2:3], first, last_, ALU.not_equal)
            dve.tensor_tensor(cols[:, 3:4], df[:, 2, T - 1:T], first, ALU.not_equal).then_inc(s_prep.sem, 1)
            dve.wait_ge(s_prep.sem, next(order))
            dve.tensor_reduce(ends_cnt[:, 0:1], in_first[:], AX.X, ALU.add)
            dve.tensor_reduce(ends_cnt[:, 1:2], in_last[:], AX.X, ALU.add)
            dve.tensor_copy(cols[:, 0:1], same[:, 0:1])
            dve.tensor_copy(cols[:, 1:2], tmpa[:, T - 1:T])
            dve.tensor_scalar(rep[:], tmpa[:], -1.0, 1.0, ALU.mult, ALU.add).then_inc(s_prep.sem, 1)
            dve.wait_ge(s_prep.sem, next(order))
            dve.memset(same[:, 0:1], 0.0)
            dve.tensor_scalar(in_first[:], in_first[:], cols[:, 0:1], None, ALU.mult)
            dve.tensor_scalar(in_last[:], in_last[:], cols[:, 1:2], None, ALU.mult)
            dve.tensor_tensor(cols[:, 4:5], cols[:, 0:1], cols[:, 3:4], ALU.mult).then_inc(s_prep.sem, 1)
            dve.wait_ge(s_prep.sem, next(order))
            dve.tensor_scalar(scan[:, 0, :], same[:], -1.0, 1.0, ALU.mult, ALU.add)
            dve.tensor_scalar(scanb[:, 0, :], in_first[:], -1.0, 1.0, ALU.mult, ALU.add)
            dve.scalar_tensor_tensor(out=scan[:, 1, :], in0=tmpa[:], scalar=1024.0, in1=col[:],
                                     op0=ALU.mult, op1=ALU.add).then_inc(s_prep.sem, 1)
            dve.wait_ge(s_prep.sem, next(order))
            dve.memset(scan[:, 1, T - 1:T], float(T - 1))
            dve.tensor_tensor(rep[:], rep[:], scanb[:, 0, :], ALU.mult)
            dve.tensor_tensor(scan[:, 0, :], scan[:, 0, :], col[:], ALU.mult).then_inc(s_prep.sem, 1)
            dve.wait_ge(s_prep.sem, next(order))
            k, a, b = 1, scan, scanb
            while k < T:
                dve.tensor_copy(b[:, 0, 0:k], a[:, 0, 0:k])
                dve.tensor_tensor(b[:, 0, k:T], a[:, 0, k:T], a[:, 0, 0:T - k], ALU.max)
                dve.tensor_copy(b[:, 1, T - k:T], a[:, 1, T - k:T])
                dve.tensor_tensor(b[:, 1, 0:T - k], a[:, 1, 0:T - k], a[:, 1, k:T], ALU.min).then_inc(s_prep.sem, 1)
                dve.wait_ge(s_prep.sem, next(order))
                k, a, b = 2 * k, b, a
            dve.tensor_tensor(tmpa[:], col[:], a[:, 0, :], ALU.subtract).then_inc(s_prep.sem, 1)
            dve.wait_ge(s_prep.sem, next(order))
            dve.tensor_scalar(pay[:, :, 1], tmpa[:], 1.0, None, ALU.add)
            dve.tensor_scalar(cols[:, 9:10], cols[:, 8:9], float(T), None, ALU.mult).then_inc(s_prep.sem, 1)
            dve.wait_ge(s_prep.sem, next(order))
            dve.tensor_scalar(base[:], a[:, 1, :], cols[:, 9:10], None, ALU.add)
            dve.tensor_scalar(pay[:, :, 0], col[:], cols[:, 9:10], None, ALU.add).then_inc(s_prep.sem, 1)
            dve.wait_ge(s_prep.sem, next(order))
            dve.wait_ge(s_row.sem, 1)
            dve.tensor_copy(first_row[:], TPS[0][:, 0:P]).then_inc(s_prep.sem, 1)
            dve.wait_ge(s_prep.sem, next(order))
            dve.tensor_scalar(eq_ff[:], first_row[:], first, None, ALU.is_equal)
            dve.tensor_scalar(eq_lf[:], first_row[:], last_, None, ALU.is_equal).then_inc(s_prep.sem, 1)
            dve.wait_ge(s_prep.sem, next(order))
            dve.tensor_tensor(masked[:], eq_ff[:], part[:], ALU.mult)
            dve.tensor_tensor(masked2[:], eq_lf[:], part[:], ALU.mult).then_inc(s_prep.sem, 1)
            dve.wait_ge(s_prep.sem, next(order))
            dve.tensor_scalar(eq_lf[:], eq_lf[:], cols[:, 2:3], None, ALU.mult).then_inc(s_cntin.sem, 1)
            dve.tensor_reduce(cols[:, 5:6], masked[:], AX.X, ALU.max)
            dve.tensor_reduce(cols[:, 6:7], masked2[:], AX.X, ALU.max).then_inc(s_prep.sem, 1)
            dve.wait_ge(s_prep.sem, next(order))
            for cc, mask in ((5, in_first), (6, in_last)):
                dve.tensor_scalar(cols[:, cc + 5:cc + 6], cols[:, cc:cc + 1], float(FIX), None, ALU.add)
                dve.tensor_scalar(scan[:, 2, :], base[:], -1.0, None, ALU.mult).then_inc(s_prep.sem, 1)
                dve.wait_ge(s_prep.sem, next(order))
                dve.tensor_scalar(scan[:, 3, :], scan[:, 2, :], cols[:, cc + 5:cc + 6], None, ALU.add
                    ).then_inc(s_prep.sem, 1)
                dve.wait_ge(s_prep.sem, next(order))
                dve.tensor_tensor(scan[:, 2, :], scan[:, 3, :], mask[:], ALU.mult).then_inc(s_prep.sem, 1)
                dve.wait_ge(s_prep.sem, next(order))
                dve.tensor_tensor(base[:], base[:], scan[:, 2, :], ALU.add).then_inc(s_prep.sem, 1)
                dve.wait_ge(s_prep.sem, next(order))
            dve.tensor_copy(idx[:, :, 3], base[:])
            dve.tensor_copy(idx[:, :, 0], si[:])
            dve.tensor_scalar(idx[:, :, 1], own, float(N - 1), None, ALU.min)
            dve.tensor_scalar(idx_fix[:, 0:1], first, float(N - 1), None, ALU.min)
            dve.tensor_scalar(cols[:, 12:13], first, -float(SKIP), None, ALU.add)
            dve.tensor_tensor(cols[:, 13:14], cols[:, 9:10], ends_cnt[:, 0:1], ALU.add)
            dve.tensor_scalar(pay_fix[:, 0:1], cols[:, 8:9], float(FIX), None, ALU.add)
            dve.tensor_scalar(tmpa[:], own, -float(SKIP), None, ALU.add).then_inc(s_prep.sem, 1)
            dve.wait_ge(s_prep.sem, next(order))
            dve.tensor_tensor(cols[:, 14:15], cols[:, 12:13], cols[:, 4:5], ALU.mult)
            dve.tensor_scalar(idx_fix[:, 2:3], cols[:, 13:14], -1.0, None, ALU.add)
            dve.tensor_tensor(scan[:, 0, :], tmpa[:], rep[:], ALU.mult).then_inc(s_prep.sem, 1)
            dve.wait_ge(s_prep.sem, next(order))
            dve.tensor_scalar(idx[:, :, 4], scan[:, 0, :], float(SKIP), None, ALU.add)
            dve.tensor_scalar(idx_fix[:, 1:2], cols[:, 14:15], float(SKIP), None, ALU.add)
            dve.wait_ge(s_cnt.sem, 1)
            dve.tensor_copy(pay_fix[:, 1:2], QS[1][:, 0:1]).then_inc(s_idx.sem, 1)

            def degrees():
                dve.wait_ge(s_seen.sem, EU)
                dve.tensor_copy(idx[:, :, 2], seen[:, :, 0])
                dve.tensor_scalar(degs[:, 0:T], seen[:, :, 1], 1.0, None, ALU.add)
                dve.tensor_scalar(degs[:, T:2 * T], pay[:, :, 1], 1.0, None, ALU.add)
                dve.wait_ge(s_idx.sem, 1)
                dve.tensor_scalar(degs[:, 2 * T:], pay_fix[:, 1:2], 1.0, None, ALU.add).then_inc(s_deg.sem, 1)

            def factors():
                dve.wait_ge(s_deg.sem, 1)
                steps = count(1)
                dve.tensor_scalar(dis_t[:].bitcast(I32), degs[:].bitcast(I32), 1, None,
                                  ALU.logical_shift_right).then_inc(s_dis.sem, 1)
                dve.wait_ge(s_dis.sem, next(steps))
                dve.tensor_scalar(dis[:].bitcast(I32), dis_t[:].bitcast(I32), -1, 0x5f3759df, ALU.mult,
                                  ALU.add).then_inc(s_dis.sem, 1)
                dve.wait_ge(s_dis.sem, next(steps))
                for _ in range(3):
                    dve.tensor_tensor(dis_t[:], dis[:], dis[:], ALU.mult).then_inc(s_dis.sem, 1)
                    dve.wait_ge(s_dis.sem, next(steps))
                    dve.scalar_tensor_tensor(out=dis_t[:], in0=dis_t[:], scalar=-0.5, in1=degs[:],
                                             op0=ALU.mult, op1=ALU.mult).then_inc(s_dis.sem, 1)
                    dve.wait_ge(s_dis.sem, next(steps))
                    dve.scalar_tensor_tensor(out=dis[:], in0=dis_t[:], scalar=1.5, in1=dis[:],
                                             op0=ALU.add, op1=ALU.mult).then_inc(s_dis.sem, 1)
                    dve.wait_ge(s_dis.sem, next(steps))
                dve.tensor_copy(fac[:, :, 0], dis[:, 0:T])
                dve.tensor_copy(fac[:, :, 1], dis[:, T:2 * T])
                dve.tensor_tensor(fac[:, :, 2], dis[:, T:2 * T], degs[:, T:2 * T], ALU.mult)
                dve.tensor_copy(fac[:, :, 3], same[:])
                dve.reciprocal(fac[:, :, 4], pay[:, :, 1])
                dve.memset(fac_fix[:, 0:1], 0.0)
                dve.memset(fac_fix[:, 3:4], 0.0)
                dve.tensor_copy(fac_fix[:, 1:2], dis[:, 2 * T:])
                dve.tensor_tensor(fac_fix[:, 2:3], dis[:, 2 * T:], degs[:, 2 * T:], ALU.mult)
                dve.reciprocal(fac_fix[:, 4:5], pay_fix[:, 1:2]).then_inc(s_fac.sem, 1)
                dve.wait_ge(s_fac.sem, 1)

            def stats(c, b, sets, u):
                w = u.c % 2
                bn, tmp = c.bn[b], c.tmp
                per, o3_ = (3, 0) if c is e2 else (6, 3 * b)
                for o, tiles, m in sets:
                    for g in range(m):
                        i = dve.bn_stats(bn[:, o + g, :], tiles[:, g, :])
                i.then_inc(c.s_stats.sem, 1)
                dve.wait_ge(c.s_stats.sem, u.times(per, o3_ + 1))
                dve.tensor_tensor(tmp[:, 0, :], bn[:, :, 1], bn[:, :, 4], ALU.subtract)
                dve.tensor_tensor(tmp[:, 1, :], bn[:, :, 1], bn[:, :, 4], ALU.add)
                dve.scalar_tensor_tensor(out=tmp[:, 2, :], in0=bn[:, :, 2], scalar=D * EPS, in1=bn[:, :, 5],
                                         op0=ALU.add, op1=ALU.add).then_inc(c.s_stats.sem, 1)
                dve.wait_ge(c.s_stats.sem, u.times(per, o3_ + 2))
                dve.scalar_tensor_tensor(out=tmp[:, 0, :], in0=tmp[:, 0, :], scalar=0.25, in1=tmp[:, 0, :],
                                         op0=ALU.mult, op1=ALU.mult)
                dve.tensor_scalar(c.nmean[b][:, w, :], tmp[:, 1, :], -0.5, None, ALU.mult).then_inc(c.s_stats.sem, 1)
                dve.wait_ge(c.s_stats.sem, u.times(per, o3_ + 3))
                dve.scalar_tensor_tensor(out=c.var[b][:, w, :], in0=tmp[:, 2, :], scalar=1.0 / D,
                                         in1=tmp[:, 0, :], op0=ALU.mult, op1=ALU.add).then_inc(c.s_var[b].sem, 1)

            def deviation(c, w):
                dve.tensor_tensor(c.u[:, w, :, D], c.var[0][:, w, 0:G], c.rstd[0][:, w, 0:G],
                                  ALU.mult).then_inc(c.s_u.sem, 1)

            def neg_mean(c, u, w):
                dve.tensor_tensor(c.nb[:, w, :], c.nmean[0][:, w, G:2 * G], c.rstd[0][:, w, G:2 * G],
                                  ALU.mult).then_inc(c.s_nb.sem, 1)

            def add_be1(c, u, m=G):
                i = dve.tensor_tensor(c.xb[:, 0:m], c.x[:, u.slot, 0:m],
                                      be1b[:, :].unsqueeze(1).broadcast_to([P, m, D]), ALU.add)
                if c is node:
                    i.then_inc(c.s_xb.sem, 1)

            def scaled_a2(c, u, b, o, w, m=G):
                if c is edge:
                    add_be1(c, u, m)
                for g in range(m):
                    i = dve.scalar_tensor_tensor(out=c.z[:, g, :], in0=c.a2[:, u.c % c.a2.shape[1], g, :],
                                                 scalar=c.nmean[b][:, w, o + g:o + g + 1], in1=g1b[:, :],
                                                 op0=ALU.add, op1=ALU.mult)
                i.then_inc(c.s_z.sem, 1)

            def apply_x1(c, u, b, o, w, m=G):
                dve.wait_ge(c.s_z.sem, c.s_z.upto(u))
                if c is e2:
                    dve.wait_ge(c.s_xb.sem, c.s_xb.upto(u))
                    if (u - R).exists:
                        dve.wait_ge(c.s_o.sem, c.s_o.upto(u - R))
                for g in range(m):
                    i = dve.scalar_tensor_tensor(out=c.x1[:, u.slot, g, :], in0=c.z[:, g, :],
                                                 scalar=c.rstd[b][:, w, o + g:o + g + 1], in1=c.xb[:, g, :],
                                                 op0=ALU.mult, op1=ALU.add)
                i.then_inc(c.s_x1.sem, 1)

            def add_out(c, u, m=G):
                dve.wait_ge(c.s_h.sem, c.s_h.upto(u))
                if (u - R).exists:
                    dve.wait_ge(c.o_stored[(u - R).slot], c.o_stored.upto(u - R))
                dve.tensor_tensor(c.o[:, u.slot, 0:m], c.x1[:, u.slot, 0:m], c.h[:, u.slot, 0:m],
                                  ALU.add).then_inc(c.s_o.sem, 1)

            def running_sum(sums_, fct_, msg_, u, counted):
                for g in range(G):
                    before = sums_[:, u.slot, g - 1, :] if g else sums_[:, (u.c - 1) % R, G - 1, :]
                    if u.number == 0 and g == 0:
                        dve.tensor_copy(sums_[:, 0, 0, :], msg_[:, 0, :]).then_inc(counted.sem, 1)
                    else:
                        dve.scalar_tensor_tensor(out=sums_[:, u.slot, g, :], in0=before,
                                                 scalar=fct_[:, u.c % 2, g, 3:4], in1=msg_[:, g, :],
                                                 op0=ALU.mult, op1=ALU.add).then_inc(counted.sem, 1)
                    dve.wait_ge(counted.sem, counted.at(u.times(G, g + 1)))

            def factors_of(fct_, u, counted):
                if u.number == EU:
                    i = dve.tensor_copy(fct_[:, u.c % 2, 0, :], fac_fix[:, :])
                else:
                    i = dve.tensor_copy(fct_[:, u.c % 2], fac[:, bass.ds(u.times(G), G), :])
                i.then_inc(counted.sem, 1)
                dve.wait_ge(counted.sem, counted.upto(u))

            def chain_stats(c, t, n):
                v, e1 = (t.c - 1) % 2, c is edge
                late = c.late
                if not t.within(n + 3 + late):
                    return
                fix = 1 if t.number == n else G
                sets = []
                if t.within(n):
                    dve.wait_ge(c.loaded[t.slot], c.loaded.upto(t, 16 * G if e1 else 16))
                    sets.append((0, c.x[:, t.slot], G))
                if e1 and t.within(n + 1):
                    dve.wait_ge(xd_loaded[t.slot], xd_loaded.upto(t, 16 * G, 16 * fix))
                    sets.append((2 * G, xd[:, t.slot], fix))
                u = t - 3 - late
                if u.within(n):
                    dve.wait_ge(c.s_x1.sem, c.s_x1.upto(u))
                    sets.append((G, c.x1[:, u.slot], G))
                stats(c, 0, sets, t)
                if c is node and (t - 2 - late).within(n):
                    add_be1(c, t - 2 - late)
                b_on = t.within(n + 2 + late)
                sets = []
                if (t - 1).within(n):
                    dve.wait_ge(c.s_a1.sem, c.s_a1.upto(t - 1))
                    sets.append((0, c.a1[:, v, :, 0:D], G))
                if e1 and (t - 1).within(n + 1):
                    dve.wait_ge(s_ad.sem, s_ad.upto(t - 1))
                    sets.append((2 * G, ad[:, v, :, 0:D], 1 if (t - 1).number == n else G))
                u = t - 2 - late
                if u.within(n):
                    dve.wait_ge(c.s_a2.sem, c.s_a2.upto(u))
                    sets.append((G, c.a2[:, u.c % c.a2.shape[1]], G))
                if b_on:
                    if sets:
                        stats(c, 1, sets, t)
                    else:
                        stats(c, 1, [(0, g1b[:, :].unsqueeze(1), 1)], t)

            def chain_apply(c, t, n):
                w, v = t.c % 2, (t.c - 1) % 2
                e1 = c is edge
                late = c.late
                on, b_on = t.within(n + 3 + late), t.within(n + 2 + late)
                if not on:
                    if (t - 4 - late).within(n) and not e1:
                        add_out(c, t - 4 - late)
                    return
                fix = 1 if t.number == n else G
                dve.wait_ge(c.s_rstd[0].sem, c.s_rstd[0].upto(t))
                if t.within(n):
                    deviation(c, w)
                if (t - 3 - late).within(n):
                    neg_mean(c, t - 3 - late, w)
                if e1 and t.within(n + 1):
                    sums_of_unit(t, n, w, fix)
                if (t - 4 - late).within(n) and not e1:
                    add_out(c, t - 4 - late)
                if not b_on:
                    return
                if (t - 2 - late).within(n):
                    scaled_a2(c, t - 2 - late, 1, G, w)
                dve.wait_ge(c.s_rstd[1].sem, c.s_rstd[1].upto(t))
                if (t - 1).within(n):
                    if e1:
                        dve.tensor_copy(c.a1[:, v, :, DA], c.rstd[1][:, w, 0:G])
                    dve.tensor_tensor(c.a1[:, v, :, D], c.var[1][:, w, 0:G], c.rstd[1][:, w, 0:G],
                                      ALU.mult).then_inc(c.s_a1_std.sem, 1)
                if (t - 2 - late).within(n):
                    apply_x1(c, t - 2 - late, 1, G, w)
                if e1 and (t - 1).within(n + 1):
                    m = 1 if (t - 1).number == n else G
                    o = slice(2 * G, 2 * G + m)
                    dve.tensor_copy(ad[:, v, 0:m, DA], c.rstd[1][:, w, o])
                    dve.tensor_tensor(ad[:, v, 0:m, D], c.var[1][:, w, o], c.rstd[1][:, w, o],
                                      ALU.mult).then_inc(s_zd.sem, 1)

            def sums_of_unit(t, n, w, m):
                c = edge
                factors_of(fct, t, s_fct)
                if m == G:
                    dve.tensor_tensor(coef[:, w, 0, :], c.rstd[0][:, w, 0:G], fct[:, w, :, 0], ALU.mult)
                dve.tensor_tensor(coef[:, w, 1, 0:m], c.rstd[0][:, w, 2 * G:2 * G + m], fct[:, w, 0:m, 1],
                                  ALU.mult).then_inc(s_coef.sem, 1)
                dve.wait_ge(s_coef.sem, s_coef.upto(t))
                dve.wait_ge(s_ud.sem, s_ud.upto(t))
                if m == G:
                    dve.wait_ge(c.s_relu.sem, c.s_relu.upto(t))
                    for g in range(G):
                        i = dve.tensor_scalar(msg[:, g, :], c.u[:, w, g, 0:D], coef[:, w, 0, g:g + 1], None,
                                              ALU.mult)
                    i.then_inc(s_msg.sem, 1)
                    dve.wait_ge(s_msg.sem, s_msg.upto(t))
                    if (t - R).exists:
                        dve.wait_ge(sum_stored[(t - R).slot], sum_stored.upto(t - R))
                    running_sum(sums, fct, msg, t, s_sum)
                else:
                    dve.wait_ge(s_tot.sem, 1)
                for g in range(m):
                    total = sums[:, t.slot, g, :] if m == G else QS[3][:, 4 * D:5 * D]
                    dve.scalar_tensor_tensor(out=bd[:, w, g, 0:D], in0=ud[:, g, :],
                                             scalar=coef[:, w, 1, g:g + 1], in1=total, op0=ALU.mult,
                                             op1=ALU.add)
                dve.tensor_copy(bd[:, w, 0:m, D], fct[:, w, 0:m, 2]).then_inc(s_bd.sem, 1)

            def stats2(t):
                c = e2
                if t.number == 0:
                    dve.wait_ge(edge.s_h.sem, edge.s_h.upto(At(None, EU - 1)))
                if t.within(EU + 3, 1):
                    k = t - 1
                    sets = []
                    if k.within(EU + 1):
                        dve.wait_ge(c.s_a2.sem, c.s_a2.upto(k))
                        sets.append((0, c.a2[:, k.c % 2], 1 if k.number == EU else G))
                    if (t - 2).within(EU + 1):
                        dve.wait_ge(c.s_x1.sem, c.s_x1.upto(t - 2))
                        sets.append((G, c.x1[:, (t - 2).slot], 1 if (t - 2).number == EU else G))
                    stats(c, 0, sets, k)

            def chain2(t):
                c, w = e2, t.c % 2
                if t.within(EU + 1):
                    m = 1 if t.number == EU else G
                    factors_of(fct2, t, s_fct2)
                    dve.wait_ge(zd2_loaded[t.slot], zd2_loaded.upto(t))
                    i = dve.tensor_tensor(coef2[:, w, 1, 0:m], fct2[:, w, 0:m, 1], zd2[:, t.slot, 0:m, DA], ALU.mult)
                    if m == G:
                        dve.wait_ge(zs2_laid[t.slot], zs2_laid.upto(t, 16 * G))
                        i = dve.tensor_tensor(coef2[:, w, 0, :], fct2[:, w, :, 0], zs2[:, t.slot, :, DA], ALU.mult)
                    i.then_inc(s_coef2.sem, 1)
                    dve.wait_ge(s_coef2.sem, s_coef2.upto(t))
                    if m == G:
                        for g in range(G):
                            i = dve.tensor_scalar(msg2[:, g, :], zs2[:, t.slot, g, 0:DA], coef2[:, w, 0, g:g + 1],
                                                  None, ALU.mult)
                        i.then_inc(s_msg2.sem, 1)
                        dve.wait_ge(s_msg2.sem, s_msg2.upto(t))
                        if (t - R).exists:
                            dve.wait_ge(sum2_stored[(t - R).slot], sum2_stored.upto(t - R))
                        running_sum(sums2, fct2, msg2, t, s_sum2)
                    else:
                        dve.wait_ge(s_tot.sem, 2)
                    for g in range(m):
                        total = sums2[:, t.slot, g, :] if m == G else QS[3][:, 4 * D:4 * D + DA]
                        dve.scalar_tensor_tensor(out=c.u[:, w, g, 0:DA], in0=zd2[:, t.slot, g, 0:DA],
                                                 scalar=coef2[:, w, 1, g:g + 1], in1=total, op0=ALU.mult,
                                                 op1=ALU.add)
                    dve.tensor_copy(c.u[:, w, 0:m, DA], fct2[:, w, 0:m, 2]).then_inc(c.s_u.sem, 1)
                if t.within(EU + 3, 1):
                    k = t - 1
                    if k.within(EU + 1):
                        scaled_a2(c, k, 0, 0, k.c % 2, 1 if k.number == EU else G)
                    dve.wait_ge(c.s_rstd[0].sem, c.s_rstd[0].upto(k))
                    if k.within(EU + 1):
                        apply_x1(c, k, 0, 0, k.c % 2, 1 if k.number == EU else G)
                    if (t - 2).within(EU + 1):
                        neg_mean(c, t - 2, k.c % 2)

            def step(s):
                a, b = s - S1, s - S2
                chain_stats(node, s, NU)
                chain_stats(edge, a, EU)
                stats2(b)
                chain_apply(node, s, NU)
                chain_apply(edge, a, EU)
                chain2(b)
                if s.number == S1 - 2:
                    degrees()
                if s.number == S1 - 1:
                    factors()

            run_steps(dve, step)

            def copy_attr(u):
                dve.wait_ge(s_tp3.sem, s_tp3.upto(u))
                if (u - 1).exists:
                    dve.wait_ge(s_q3.sem, s_q3.upto(u - 1))
                dve.tensor_copy(ut[0:DE, 2, :], TPS[2][0:DE, :]).then_inc(s_ut3.sem, 1)

            def step3(u):
                if not u.within(EU + 1):
                    return
                fix = u.number == EU
                factors_of(fct3, u, s_fct3)
                if u.number == 0:
                    copy_attr(u)
                if (u + 1).within(EU):
                    copy_attr(u + 1)
                if not fix:
                    q = QALL[:, 1024 * (u.c % 2):1024 * (u.c % 2) + 1024].rearrange(
                        "p (b f) -> p b f", b=2)[:, :, 0:4 * D].rearrange("p b (g f) -> p b g f", g=2)
                    dve.wait_ge(s_exp3.sem, s_exp3.upto(u))
                    dve.tensor_scalar(eg3[:], eg3[:], 1.0, None, ALU.add).then_inc(s_e13.sem, 1)
                    dve.wait_ge(s_e13.sem, s_e13.upto(u))
                    dve.reciprocal(gt3[:], eg3[:]).then_inc(s_rc3.sem, 1)
                    dve.wait_ge(s_ln3.sem, s_ln3.upto(u))
                    for b in range(2):
                        i = dve.scalar_tensor_tensor(out=ab3[:, 2 * b:2 * b + 2, :], in0=q[:, b, :, D:2 * D],
                                                     scalar=0.0, in1=ln3[:, 2 * b:2 * b + 2, :],
                                                     op0=ALU.max, op1=ALU.add)
                    i.then_inc(s_m3.sem, 1)
                    dve.wait_ge(s_m3.sem, s_m3.upto(u))
                    dve.wait_ge(s_rc3.sem, s_rc3.upto(u))
                    dve.tensor_tensor(msg[:], ab3[:], gt3[:], ALU.mult).then_inc(s_gt3.sem, 1)
                    dve.wait_ge(s_gt3.sem, s_gt3.upto(u))
                    if (u - R).exists:
                        dve.wait_ge(sum3_stored[(u - R).slot], sum3_stored.upto(u - R))
                    running_sum(sums3, fct3, msg, u, s_sum3)
                    dve.wait_ge(rest3_loaded[u.slot], rest3_loaded.upto(u, 32))
                else:
                    dve.wait_ge(s_tot.sem, 3)
                    dve.wait_ge(rest3_loaded[u.slot], rest3_loaded.upto(u, 32, 16))
                m = 1 if fix else G
                if (u - R).exists:
                    dve.wait_ge(out_put[(u - R).slot], out_put.upto(u - R, 16 * G))
                for g in range(m):
                    total = QS[3][:, 4 * D:5 * D] if fix else sums3[:, u.slot, g, :]
                    i = dve.scalar_tensor_tensor(out=res3[:, u.slot, g, :], in0=total,
                                                 scalar=fct3[:, u.c % 2, g, 4:5], in1=o3[:, u.slot, g, :],
                                                 op0=ALU.mult, op1=ALU.add)
                i.then_inc(s_res3.sem, 1)

            run_steps(dve, step3, SEGMENTS3)


_INS = ["x", "src", "dst", "edge_attr_64", "L0_gnn_W0", "L0_gnn_b0", "L0_gnn_g0", "L0_gnn_be0",
        "L0_gnn_W1", "L0_gnn_b1", "L0_gnn_g1", "L0_gnn_be1", "L1_gnn_W_e", "L1_gnn_b_e",
        "L1_gnn_W_n", "L1_gnn_b_n"]


def kernel(**inputs):
    import numpy as _np
    import concourse.bacc as _bacc
    from concourse import mybir as _mybir
    from concourse.bass_utils import run_bass_kernel_spmd as _run

    nc = _bacc.Bacc("TRN2", target_bir_lowering=False, num_devices=1)
    arrays, args = {}, []
    for name in _INS:
        a = _np.ascontiguousarray(inputs[name])
        arrays[f"in_{name}_dram"] = a
        args.append(nc.dram_tensor(f"in_{name}_dram", a.shape, _mybir.dt.from_np(a.dtype),
                                   kind="ExternalInput").ap())
    args.append(nc.dram_tensor("out_0_dram", (N, D), F32, kind="ExternalOutput").ap())
    build(nc, *args)
    r = _run(nc, [arrays], core_ids=[0])
    return r.results[0]["out_0_dram"]
```
